# Optimizing a Trainium2 kernel written in Bass

```python
import numpy as np
import jax
import jax.numpy as jnp

def _softmax(x, axis=-1):
    return jax.nn.softmax(x, axis=axis)

def _gelu(x):
    return jax.nn.gelu(x, approximate=True)

def _silu(x):
    return jax.nn.silu(x)

def _sigmoid(x):
    return jax.nn.sigmoid(x)

def _layernorm(x, axis=-1, eps=1e-05):
    m = jnp.mean(x, axis=axis, keepdims=True)
    v = jnp.var(x, axis=axis, keepdims=True)
    return (x - m) / jnp.sqrt(v + eps)

def _scatter_add(tgt, idx, src, axis=0):
    return tgt.at[idx].add(src)

def _segment_sum(src, seg, n):
    return jax.ops.segment_sum(src, seg, n)
kernel_name = 'mk_seq_preln_d1_jaxref_r8_34a9e8'

def setup_inputs(seed: int=0):
    np.random.seed(seed)
    _w = jnp.asarray

    def _L0_attn_setup():
        import math
        import jax, jax.numpy as jnp
        import numpy as np
        D_MODEL = 128
        N_HEADS = 16
        D_HEAD = D_MODEL // N_HEADS
        SEQ = 512
        BATCH = 1
        BASE = 10000.0
        EPS = 1e-05

        def _layernorm(x, g, b):
            mu = jnp.mean(x, axis=-1, keepdims=True)
            var = jnp.mean(jnp.square(x - mu), axis=-1, keepdims=True)
            return (x - mu) * jax.lax.rsqrt(var + EPS) * g + b

        def _rotate(x, cos, sin):
            b, H, n, dh = x.shape
            xr = x.reshape(b, H, n, dh // 2, 2)
            x1, x2 = (xr[..., 0], xr[..., 1])
            r1 = x1 * cos - x2 * sin
            r2 = x1 * sin + x2 * cos
            return jnp.stack([r1, r2], axis=-1).reshape(b, H, n, dh)

        def _block(x, ln1_g, ln1_b, ln2_g, ln2_b, Wqkv, Wo, W1, b1, W2, b2):
            b, n, d = x.shape
            H, dh = (N_HEADS, D_HEAD)
            h = _layernorm(x, ln1_g, ln1_b)
            qkv = (h @ Wqkv).reshape(b, n, 3, H, dh)
            q = jnp.transpose(qkv[:, :, 0], (0, 2, 1, 3))
            k = jnp.transpose(qkv[:, :, 1], (0, 2, 1, 3))
            v = jnp.transpose(qkv[:, :, 2], (0, 2, 1, 3))
            inv_freq = BASE ** (-(jnp.arange(0, dh, 2, dtype=jnp.float32) / dh))
            theta = jnp.arange(n, dtype=jnp.float32)[:, None] * inv_freq[None, :]
            cos, sin = (jnp.cos(theta), jnp.sin(theta))
            q = _rotate(q, cos, sin)
            k = _rotate(k, cos, sin)
            s = jnp.einsum('bhqd,bhkd->bhqk', q, k) / math.sqrt(dh)
            causal = jnp.tril(jnp.ones((n, n), dtype=bool))
            s = jnp.where(causal, s, -jnp.inf)
            a = jax.nn.softmax(s, axis=-1)
            o = jnp.einsum('bhqk,bhkd->bqhd', a, v).reshape(b, n, d)
            x = x + o @ Wo
            h2 = _layernorm(x, ln2_g, ln2_b)
            f = jax.nn.gelu(h2 @ W1 + b1, approximate=False) @ W2 + b2
            return x + f
        key = jax.random.key(seed)
        ks = jax.random.split(key, 8)
        d, h = (D_MODEL, 4 * D_MODEL)
        s = 0.02
        return {'x': jax.random.normal(ks[0], (BATCH, SEQ, d), jnp.float32), 'ln1_g': jnp.ones((d,), jnp.float32), 'ln1_b': jnp.zeros((d,), jnp.float32), 'ln2_g': jnp.ones((d,), jnp.float32), 'ln2_b': jnp.zeros((d,), jnp.float32), 'Wqkv': jax.random.normal(ks[1], (d, 3 * d), jnp.float32) * s, 'Wo': jax.random.normal(ks[2], (d, d), jnp.float32) * s, 'W1': jax.random.normal(ks[3], (d, h), jnp.float32) * s, 'b1': jnp.zeros((h,), jnp.float32), 'W2': jax.random.normal(ks[4], (h, d), jnp.float32) * s, 'b2': jnp.zeros((d,), jnp.float32)}
    _L0_attn_in = _L0_attn_setup()

    def _L0_ffn_setup():
        import jax, jax.numpy as jnp
        import numpy as np
        from math import sqrt
        B, S, D, H, E, K, FF = (2, 128, 128, 16, 8, 2, 512)
        HD = D // H
        EPS = 1e-05

        def _rope_cache(seq_len, hd):
            inv_freq = 1.0 / 10000.0 ** (jnp.arange(0, hd, 2, dtype=jnp.float32) / hd)
            t = jnp.arange(seq_len, dtype=jnp.float32)
            freqs = t[:, None] * inv_freq[None, :]
            emb = jnp.concatenate([freqs, freqs], axis=-1)
            return (jnp.cos(emb), jnp.sin(emb))

        def _rotate_half(x):
            x1, x2 = jnp.split(x, 2, axis=-1)
            return jnp.concatenate([-x2, x1], axis=-1)

        def _layernorm(x, g, b):
            m = jnp.mean(x, axis=-1, keepdims=True)
            v = jnp.var(x, axis=-1, keepdims=True)
            return (x - m) * jax.lax.rsqrt(v + EPS) * g + b

        def _forward(x, Wq, bq, Wk, bk, Wv, bv, Wo, bo, Wg, bg, W1, b1, W2, b2, g1, be1, g2, be2):
            bsz, seq, d = x.shape
            q = (x @ Wq + bq).reshape(bsz, seq, H, HD).transpose(0, 2, 1, 3)
            k = (x @ Wk + bk).reshape(bsz, seq, H, HD).transpose(0, 2, 1, 3)
            v = (x @ Wv + bv).reshape(bsz, seq, H, HD).transpose(0, 2, 1, 3)
            cos, sin = _rope_cache(seq, HD)
            cos = cos[None, None]
            sin = sin[None, None]
            q = q * cos + _rotate_half(q) * sin
            k = k * cos + _rotate_half(k) * sin
            scores = jnp.einsum('bhqd,bhkd->bhqk', q, k) / sqrt(HD)
            attn = jax.nn.softmax(scores, axis=-1)
            ao = jnp.einsum('bhqk,bhkd->bhqd', attn, v)
            ao = ao.transpose(0, 2, 1, 3).reshape(bsz, seq, d)
            attn_out = ao @ Wo + bo
            x1 = _layernorm(x + attn_out, g1, be1)
            gate_logits = x1 @ Wg + bg
            gate_probs = jax.nn.softmax(gate_logits, axis=-1)
            topk_p, topk_i = jax.lax.top_k(gate_probs, K)
            topk_p = topk_p / jnp.sum(topk_p, axis=-1, keepdims=True)
            comb = jnp.sum(jax.nn.one_hot(topk_i, E, dtype=x.dtype) * topk_p[..., None], axis=-2)
            h = jax.nn.gelu(jnp.einsum('bsd,edf->bsef', x1, W1) + b1, approximate=False)
            y = jnp.einsum('bsef,efd->bsed', h, W2) + b2
            moe_out = jnp.einsum('bse,bsed->bsd', comb, y)
            return _layernorm(x1 + moe_out, g2, be2)
        key = jax.random.key(seed)
        ks = jax.random.split(key, 20)
        std = 0.02
        p = lambda k, sh: jax.random.normal(k, sh, dtype=jnp.float32) * std
        return {'x': jax.random.normal(ks[0], (B, S, D), dtype=jnp.float32), 'Wq': p(ks[1], (D, D)), 'bq': jnp.zeros((D,), jnp.float32), 'Wk': p(ks[2], (D, D)), 'bk': jnp.zeros((D,), jnp.float32), 'Wv': p(ks[3], (D, D)), 'bv': jnp.zeros((D,), jnp.float32), 'Wo': p(ks[4], (D, D)), 'bo': jnp.zeros((D,), jnp.float32), 'Wg': p(ks[5], (D, E)), 'bg': jnp.zeros((E,), jnp.float32), 'W1': p(ks[6], (E, D, FF)), 'b1': jnp.zeros((E, FF), jnp.float32), 'W2': p(ks[7], (E, FF, D)), 'b2': jnp.zeros((E, D), jnp.float32), 'g1': jnp.ones((D,), jnp.float32), 'be1': jnp.zeros((D,), jnp.float32), 'g2': jnp.ones((D,), jnp.float32), 'be2': jnp.zeros((D,), jnp.float32)}
    _L0_ffn_in = _L0_ffn_setup()
    _d = {'L0_attn_x': _L0_attn_in['x'], 'L0_attn_ln1_g': _L0_attn_in['ln1_g'], 'L0_attn_ln1_b': _L0_attn_in['ln1_b'], 'L0_attn_ln2_g': _L0_attn_in['ln2_g'], 'L0_attn_ln2_b': _L0_attn_in['ln2_b'], 'L0_attn_Wqkv': _L0_attn_in['Wqkv'], 'L0_attn_Wo': _L0_attn_in['Wo'], 'L0_attn_W1': _L0_attn_in['W1'], 'L0_attn_b1': _L0_attn_in['b1'], 'L0_attn_W2': _L0_attn_in['W2'], 'L0_attn_b2': _L0_attn_in['b2'], 'L0_ffn_Wq': _L0_ffn_in['Wq'], 'L0_ffn_bq': _L0_ffn_in['bq'], 'L0_ffn_Wk': _L0_ffn_in['Wk'], 'L0_ffn_bk': _L0_ffn_in['bk'], 'L0_ffn_Wv': _L0_ffn_in['Wv'], 'L0_ffn_bv': _L0_ffn_in['bv'], 'L0_ffn_Wo': _L0_ffn_in['Wo'], 'L0_ffn_bo': _L0_ffn_in['bo'], 'L0_ffn_Wg': _L0_ffn_in['Wg'], 'L0_ffn_bg': _L0_ffn_in['bg'], 'L0_ffn_W1': _L0_ffn_in['W1'], 'L0_ffn_b1': _L0_ffn_in['b1'], 'L0_ffn_W2': _L0_ffn_in['W2'], 'L0_ffn_b2': _L0_ffn_in['b2'], 'L0_ffn_g1': _L0_ffn_in['g1'], 'L0_ffn_be1': _L0_ffn_in['be1'], 'L0_ffn_g2': _L0_ffn_in['g2'], 'L0_ffn_be2': _L0_ffn_in['be2']}
    _x0 = _d['L0_attn_x']
    _d['L0_attn_x'] = jax.random.normal(jax.random.fold_in(jax.random.key(seed), 1), (4, 1024, 128), dtype=_x0.dtype)
    del _x0
    return _d

def reference(L0_attn_x, L0_attn_ln1_g, L0_attn_ln1_b, L0_attn_ln2_g, L0_attn_ln2_b, L0_attn_Wqkv, L0_attn_Wo, L0_attn_W1, L0_attn_b1, L0_attn_W2, L0_attn_b2, L0_ffn_Wq, L0_ffn_bq, L0_ffn_Wk, L0_ffn_bk, L0_ffn_Wv, L0_ffn_bv, L0_ffn_Wo, L0_ffn_bo, L0_ffn_Wg, L0_ffn_bg, L0_ffn_W1, L0_ffn_b1, L0_ffn_W2, L0_ffn_b2, L0_ffn_g1, L0_ffn_be1, L0_ffn_g2, L0_ffn_be2):

    def _L0_attn_ref(x, ln1_g, ln1_b, ln2_g, ln2_b, Wqkv, Wo, W1, b1, W2, b2):
        import math
        import jax, jax.numpy as jnp
        import numpy as np
        D_MODEL = 128
        N_HEADS = 16
        D_HEAD = D_MODEL // N_HEADS
        SEQ = 512
        BATCH = 1
        BASE = 10000.0
        EPS = 1e-05

        def _layernorm(x, g, b):
            mu = jnp.mean(x, axis=-1, keepdims=True)
            var = jnp.mean(jnp.square(x - mu), axis=-1, keepdims=True)
            return (x - mu) * jax.lax.rsqrt(var + EPS) * g + b

        def _rotate(x, cos, sin):
            b, H, n, dh = x.shape
            xr = x.reshape(b, H, n, dh // 2, 2)
            x1, x2 = (xr[..., 0], xr[..., 1])
            r1 = x1 * cos - x2 * sin
            r2 = x1 * sin + x2 * cos
            return jnp.stack([r1, r2], axis=-1).reshape(b, H, n, dh)

        def _block(x, ln1_g, ln1_b, ln2_g, ln2_b, Wqkv, Wo, W1, b1, W2, b2):
            b, n, d = x.shape
            H, dh = (N_HEADS, D_HEAD)
            h = _layernorm(x, ln1_g, ln1_b)
            qkv = (h @ Wqkv).reshape(b, n, 3, H, dh)
            q = jnp.transpose(qkv[:, :, 0], (0, 2, 1, 3))
            k = jnp.transpose(qkv[:, :, 1], (0, 2, 1, 3))
            v = jnp.transpose(qkv[:, :, 2], (0, 2, 1, 3))
            inv_freq = BASE ** (-(jnp.arange(0, dh, 2, dtype=jnp.float32) / dh))
            theta = jnp.arange(n, dtype=jnp.float32)[:, None] * inv_freq[None, :]
            cos, sin = (jnp.cos(theta), jnp.sin(theta))
            q = _rotate(q, cos, sin)
            k = _rotate(k, cos, sin)
            s = jnp.einsum('bhqd,bhkd->bhqk', q, k) / math.sqrt(dh)
            causal = jnp.tril(jnp.ones((n, n), dtype=bool))
            s = jnp.where(causal, s, -jnp.inf)
            a = jax.nn.softmax(s, axis=-1)
            o = jnp.einsum('bhqk,bhkd->bqhd', a, v).reshape(b, n, d)
            x = x + o @ Wo
            h2 = _layernorm(x, ln2_g, ln2_b)
            f = jax.nn.gelu(h2 @ W1 + b1, approximate=False) @ W2 + b2
            return x + f
        return _block(x, ln1_g, ln1_b, ln2_g, ln2_b, Wqkv, Wo, W1, b1, W2, b2)

    def _L0_ffn_ref(x, Wq, bq, Wk, bk, Wv, bv, Wo, bo, Wg, bg, W1, b1, W2, b2, g1, be1, g2, be2):
        import jax, jax.numpy as jnp
        import numpy as np
        from math import sqrt
        B, S, D, H, E, K, FF = (2, 128, 128, 16, 8, 2, 512)
        HD = D // H
        EPS = 1e-05

        def _rope_cache(seq_len, hd):
            inv_freq = 1.0 / 10000.0 ** (jnp.arange(0, hd, 2, dtype=jnp.float32) / hd)
            t = jnp.arange(seq_len, dtype=jnp.float32)
            freqs = t[:, None] * inv_freq[None, :]
            emb = jnp.concatenate([freqs, freqs], axis=-1)
            return (jnp.cos(emb), jnp.sin(emb))

        def _rotate_half(x):
            x1, x2 = jnp.split(x, 2, axis=-1)
            return jnp.concatenate([-x2, x1], axis=-1)

        def _layernorm(x, g, b):
            m = jnp.mean(x, axis=-1, keepdims=True)
            v = jnp.var(x, axis=-1, keepdims=True)
            return (x - m) * jax.lax.rsqrt(v + EPS) * g + b

        def _forward(x, Wq, bq, Wk, bk, Wv, bv, Wo, bo, Wg, bg, W1, b1, W2, b2, g1, be1, g2, be2):
            bsz, seq, d = x.shape
            q = (x @ Wq + bq).reshape(bsz, seq, H, HD).transpose(0, 2, 1, 3)
            k = (x @ Wk + bk).reshape(bsz, seq, H, HD).transpose(0, 2, 1, 3)
            v = (x @ Wv + bv).reshape(bsz, seq, H, HD).transpose(0, 2, 1, 3)
            cos, sin = _rope_cache(seq, HD)
            cos = cos[None, None]
            sin = sin[None, None]
            q = q * cos + _rotate_half(q) * sin
            k = k * cos + _rotate_half(k) * sin
            scores = jnp.einsum('bhqd,bhkd->bhqk', q, k) / sqrt(HD)
            attn = jax.nn.softmax(scores, axis=-1)
            ao = jnp.einsum('bhqk,bhkd->bhqd', attn, v)
            ao = ao.transpose(0, 2, 1, 3).reshape(bsz, seq, d)
            attn_out = ao @ Wo + bo
            x1 = _layernorm(x + attn_out, g1, be1)
            gate_logits = x1 @ Wg + bg
            gate_probs = jax.nn.softmax(gate_logits, axis=-1)
            topk_p, topk_i = jax.lax.top_k(gate_probs, K)
            topk_p = topk_p / jnp.sum(topk_p, axis=-1, keepdims=True)
            comb = jnp.sum(jax.nn.one_hot(topk_i, E, dtype=x.dtype) * topk_p[..., None], axis=-2)
            h = jax.nn.gelu(jnp.einsum('bsd,edf->bsef', x1, W1) + b1, approximate=False)
            y = jnp.einsum('bsef,efd->bsed', h, W2) + b2
            moe_out = jnp.einsum('bse,bsed->bsd', comb, y)
            return _layernorm(x1 + moe_out, g2, be2)
        return _forward(x, Wq, bq, Wk, bk, Wv, bv, Wo, bo, Wg, bg, W1, b1, W2, b2, g1, be1, g2, be2)
    x = L0_attn_x
    x = x + _L0_attn_ref(_layernorm(x, axis=-1), L0_attn_ln1_g, L0_attn_ln1_b, L0_attn_ln2_g, L0_attn_ln2_b, L0_attn_Wqkv, L0_attn_Wo, L0_attn_W1, L0_attn_b1, L0_attn_W2, L0_attn_b2)
    x = x + _L0_ffn_ref(_layernorm(x, axis=-1), L0_ffn_Wq, L0_ffn_bq, L0_ffn_Wk, L0_ffn_bk, L0_ffn_Wv, L0_ffn_bv, L0_ffn_Wo, L0_ffn_bo, L0_ffn_Wg, L0_ffn_bg, L0_ffn_W1, L0_ffn_b1, L0_ffn_W2, L0_ffn_b2, L0_ffn_g1, L0_ffn_be1, L0_ffn_g2, L0_ffn_be2)
    return x

_drawn_inputs = setup_inputs


def setup_inputs(seed=0):
    import zlib

    import numpy as np

    out = dict(_drawn_inputs(seed))
    spreads = {'L0_attn_ln1_g': (1.0, 0.6),
     'L0_attn_ln1_b': (0.0, 0.8),
     'L0_attn_ln2_g': (1.0, 0.6),
     'L0_attn_ln2_b': (0.0, 2.0),
     'L0_attn_b1': (0.0, 0.644),
     'L0_attn_b2': (0.0, 0.38),
     'L0_ffn_bq': (0.0, 0.8),
     'L0_ffn_bk': (0.0, 0.8),
     'L0_ffn_bv': (0.0, 0.8),
     'L0_ffn_bo': (0.0, 0.674),
     'L0_ffn_bg': (0.0, 0.547),
     'L0_ffn_b1': (0.0, 0.8),
     'L0_ffn_b2': (0.0, 1.049),
     'L0_ffn_g1': (1.0, 0.2),
     'L0_ffn_be1': (0.0, 0.303),
     'L0_ffn_g2': (1.0, 0.2),
     'L0_ffn_be2': (0.0, 0.477)}
    factors = {'L0_attn_Wqkv': 8.0,
     'L0_attn_Wo': 8.0,
     'L0_ffn_Wq': 8.0,
     'L0_ffn_Wk': 8.0,
     'L0_ffn_Wv': 8.0,
     'L0_ffn_Wo': 6.791,
     'L0_ffn_W1': 4.383,
     'L0_ffn_W2': 3.91,
     'L0_attn_W1': 2.754}
    for name, (base, spread) in spreads.items():
        noise = np.random.default_rng([zlib.crc32(name.encode()), seed]).standard_normal(out[name].shape)
        drawn = base * np.exp(spread * noise) if base else spread * noise
        out[name] = jnp.asarray(drawn.astype(out[name].dtype))
    for name, factor in factors.items():
        out[name] = (out[name] * factor).astype(out[name].dtype)
    return out
```

```python
from contextlib import ExitStack

import numpy as np

import concourse.bass as bass
from concourse import mybir

F32 = mybir.dt.float32
BF16 = mybir.dt.bfloat16
U32 = mybir.dt.uint32
ALU = mybir.AluOpType
ACT = mybir.ActivationFunctionType
AX = mybir.AxisListType

P = 128
B, S, D = 4, 1024, 128
H, DH = 16, 8
E, FF = 8, 512
FC = FF // P
HG = 4
NG = B * H // HG
NQT = S // P
G = 512
GT = G // P
HALVES = S // G
T = B * S
EPS = 1e-5
SCALE = float(DH) ** -0.5
LOW = -3.0e38
Q_SLOTS = (0, 0, 1, 1, 0, 2)
K_SLOTS = (0, 1, 0, 1, 2, 0)
NS = len(Q_SLOTS)
KS = NS * DH
KM = KS + 3
NRING = 8
QB = 3


def at_start(i):
    return isinstance(i, int) and i == 0


def attention_plan(causal):
    chunks = []
    for qt in range(NQT):
        for kh in range(HALVES):
            width = min(G, (qt + 1) * P - kh * G) if causal else G
            if width <= 0:
                continue
            masked = causal and kh == qt // GT
            for pair in range(2):
                for par in range(2):
                    chunks.append((qt, pair, par, kh, width, masked))
    steps = []
    for qh in range(HALVES):
        n = (qh + 1) * GT if causal else NQT
        for kt in range(n):
            diagonal = causal and kt >= qh * GT
            steps.append((qh, kt, (kt - qh * GT) * P if diagonal else 0, diagonal, kt == 0, kt == n - 1))
    order, c = [], 0
    lead = 8

    def some(upto):
        nonlocal c
        while c < min(upto, len(chunks)):
            order.append(("chunk", c))
            c += 1

    some(lead)
    for k, step in enumerate(steps):
        for pair in range(2):
            order.append(("unit", 2 * k + pair))
            some(lead + (2 * k + pair + 1) * (len(chunks) - lead) // (2 * len(steps)))
        if k:
            order.append(("values", k - 1))
            if k > 2 and steps[k - 3][5]:
                order.append(("finish", steps[k - 3][0]))
    some(len(chunks))
    order.append(("values", len(steps) - 1))
    order.append(("finish", HALVES - 1))
    return chunks, steps, order


def build(nc, t, out):
    with ExitStack() as ctx:
        def sb(name, shape, dt=F32):
            return ctx.enter_context(nc.sbuf_tensor(name, shape, dt))

        def sem(name):
            return ctx.enter_context(nc.semaphore(name))

        dram = {}
        for n in (1, 2):
            for qk in "qk":
                dram[f"{qk}{n}"] = nc.dram_tensor(f"{qk}_slots{n}", [NG, 2, NS * DH, 2 * S], BF16, kind="Internal").ap()
            dram[f"o{n}"] = nc.dram_tensor(f"heads_out{n}", [NG, P, S], F32, kind="Internal").ap()
        x_ln_d = nc.dram_tensor("x_ln_d", [T, D], F32, kind="Internal").ap()
        x_mid_d = nc.dram_tensor("x_mid_d", [T, D], F32, kind="Internal").ap()
        z_d = nc.dram_tensor("z_d", [T, D], F32, kind="Internal").ap()
        x_in = t["x"].rearrange("b s d -> (b s) d")
        x_out = out.rearrange("b s d -> (b s) d")

        def tokens(dram_ap, b, half):
            return dram_ap[bass.ds(b * S + half * G, G), :].rearrange("(t p) d -> p t d", p=P)

        ident = sb("ident", [P, P])
        ident_b = sb("ident_b", [P, P], BF16)
        sel = sb("sel", [P, P])
        later_keys = sb("later_keys", [P, P], BF16)
        later_keys_T = sb("later_keys_T", [P, P], BF16)
        rope = {n: sb(f"rope{n}", [P, 2, S]) for n in (1, 2)}
        w_qk = {n: sb(f"w_qk{n}", [P, 4, P]) for n in (1, 2)}
        w_v = {n: sb(f"w_v{n}", [P, P]) for n in (1, 2)}
        w_o = {n: sb(f"w_o{n}", [P, HG, P]) for n in (1, 2)}
        b_qk = sb("b_qk", [P, 4])
        rows = sb("rows", [1, 4 + E, P])
        bg_row = sb("bg_row", [1, E])
        cols1 = sb("cols1", [P, 4])
        ln_rows = sb("ln_rows", [P, 4, P])
        w1 = sb("w1", [P, FF])
        b1c = sb("b1c", [P, FC])
        w2 = sb("w2", [P, FC, P])
        wg = sb("wg", [P, E])
        ew1 = sb("ew1", [P, E, FF])
        eb1 = sb("eb1", [P, E, FC])
        ew2 = sb("ew2", [P, E, FC, P])
        ones_row = sb("ones_row", [1, P])
        minus_half = sb("minus_half", [P, GT])
        e_base = sb("e_base", [P, GT])
        eps_col = sb("eps_col", [P, GT])
        carrier = sb("carrier", [P, 1])
        iota_e = sb("iota_e", [P, E])

        xt = sb("xt", [P, GT, D])
        xb = sb("xb", [P, GT, D])
        xc = sb("xc", [P, GT, D])
        xd = sb("xd", [P, GT, D])
        xe = sb("xe", [P, GT, D])
        xf = sb("xf", [P, GT, D])
        xz = sb("xz", [P, GT, D])
        xa = sb("xa", [P, GT, D])
        yT = sb("yT", [P, G])
        hT = sb("hT", [P, G])
        stats = sb("stats", [P, 2, GT, 6])
        mv = sb("mv", [P, 2, GT, 2])
        ve = sb("ve", [P, 2, GT])
        rstd = sb("rstd", [P, 2, GT])
        parts = sb("parts", [P, 3, 2, G], BF16)
        v_all = sb("v_all", [P, NG * NQT * HG * DH])
        gate = sb("gate", [P, GT, E])
        top = sb("top", [P, GT, 8])
        top_i = sb("top_i", [P, GT, 8], U32)
        top_f = sb("top_f", [P, GT, 2])
        gap = sb("gap", [P, GT])
        e2 = sb("e2", [P, GT])
        esum = sb("esum", [P, GT])
        pw = sb("pw", [P, GT, 2])
        comb = sb("comb", [P, 2, GT, E])

        q_rows = [sb(f"q_rows{i}", [P, 2, S], BF16) for i in range(QB)]
        k_rows = [sb(f"k_rows{i}", [P, 2, S], BF16) for i in range(QB)]
        v_ones = [sb(f"v_ones{i}", [P, NQT, HG, 32]) for i in range(QB)]
        probs = sb("probs", [P, NRING, 2, G])
        hidden = probs[:, :, 0, :].rearrange("p (h f) s -> p h f s", h=2)
        t_cos, t_sin, rot, rest = (probs[:, 2 * i:2 * i + 2, 1, :] for i in range(4))
        row_max = sb("row_max", [P, NQT, HG, HALVES])
        top_max = sb("top_max", [P, NQT * HG])
        max_rest = sb("max_rest", [P, 2, NQT * HG])
        max_parts = sb("max_parts", [P, NQT, HG, 3], BF16)
        max_T = sb("max_T", [HG * 3, S], BF16)
        o_work = sb("o_work", [P, 3, HALVES, G])
        o_sums, o_rcp, o_norm = (o_work[:, i, :, :] for i in range(3))
        heads_in = o_work[:, 0:2, :, :].rearrange("p a h s -> p (a h) s")

        banks03 = ctx.enter_context(nc.psum_tensor("banks03", [P, 4, G], F32))
        bank = [banks03[:, i, :] for i in range(4)]
        bank += [ctx.enter_context(nc.psum_tensor(f"bank{i}", [P, G], F32))[:, :] for i in range(4, 8)]

        loaded = sem("loaded")
        set_up = sem("set_up")
        phase = sem("phase")

        def barrier(eng, n):
            eng.drain().then_inc(phase, 1)
            eng.wait_ge(phase, 5 * n)

        def carry_wait(dve):
            dve.memset(carrier[:, :], 0.0)

        class Norm:

            def __init__(self, name, slot):
                self.done = sem(name)
                self.slot = slot

            def statistics(self, dve, n, src):
                i = self.slot
                if n is not None:
                    dve.wait_ge(self.done, 5 * n)
                for g in range(GT):
                    last = dve.bn_stats(stats[:, i, g, :], src[:, g, :])
                last.then_inc(self.done, 1)
                dve.wait_ge(self.done, 5 * n + 1)
                carry_wait(dve)
                for g in range(GT):
                    last = dve.bn_aggr(mv[:, i, g, :], stats[:, i, g, :])
                last.then_inc(self.done, 1)

            def root(self, pool, n):
                i = self.slot
                pool.wait_ge(self.done, 5 * n + 2)
                pool.tensor_tensor(ve[:, i, :], mv[:, i, :, 1], eps_col[:, :], ALU.add).then_inc(self.done, 1)
                pool.wait_ge(self.done, 5 * n + 3)
                pool.tensor_tensor(rstd[:, i, :], ve[:, i, :], minus_half[:, :], ALU.pow).then_inc(self.done, 1)

            def apply(self, dve, n, dst, src):
                i = self.slot
                dve.wait_ge(self.done, 5 * n + 4)
                for g in range(GT):
                    last = dve.tensor_scalar(dst[:, g, :], src[:, g, :], mv[:, i, g, 0:1], rstd[:, i, g:g + 1],
                                             ALU.subtract, ALU.mult)
                last.then_inc(self.done, 1)

        class Project:

            def __init__(self, a):
                self.a = a
                names = ("zT", "hT", "qk", "v", "v_kept", "products", "rot", "high", "rest", "middle", "low", "stored")
                self.s = {x: sem(f"project{a}_{x}") for x in names}

            def pe(self, pe, n, z, z_sem, z_value):
                s, a = self.s, self.a
                pe.wait_ge(z_sem, z_value)
                pe.wait_ge(s["hT"], n)
                for g in range(GT):
                    last = pe.transpose(bank[5][:, g * P:(g + 1) * P], z[:, g, :], ident[:, :])
                last.then_inc(s["zT"], 1)
                pe.wait_ge(s["hT"], n + 1)
                pe.wait_ge(s["products"], n)
                for i in range(4):
                    last = pe.matmul(bank[i], w_qk[a][:, i, :], hT[:, :], start=True, stop=True)
                last.then_inc(s["qk"], 1)
                pe.wait_ge(s["v_kept"], n)
                for g in range(GT):
                    o = bank[4][:, g * P:(g + 1) * P]
                    last = pe.matmul(o, hT[:, g * P:(g + 1) * P], w_v[a][:, :], start=True, stop=(a == 1))
                    if a == 2:
                        last = pe.matmul(o, ones_row[:, :], rows[:, 0, :], start=False, stop=True)
                last.then_inc(s["v"], 1)

            def dve(self, dve, n, half):
                s, a = self.s, self.a
                dve.wait_ge(s["zT"], n + 1)
                dve.wait_ge(s["v"], n)
                if a == 1:
                    dve.tensor_scalar(hT[:, :], bank[5], cols1[:, 0:1], cols1[:, 1:2], ALU.mult, ALU.add).then_inc(s["hT"], 1)
                else:
                    dve.tensor_copy(hT[:, :], bank[5]).then_inc(s["hT"], 1)
                dve.wait_ge(s["qk"], n + 1)
                dve.wait_ge(s["rot"], n)
                for i in range(4):
                    to = (t_cos, t_sin)[i % 2][:, i // 2, :]
                    table = rope[a][:, i % 2, half * G:(half + 1) * G]
                    if a == 1:
                        last = dve.tensor_tensor(to, bank[i], table, ALU.mult)
                    else:
                        last = dve.scalar_tensor_tensor(to, bank[i], b_qk[:, i:i + 1], table, ALU.add, ALU.mult)
                last.then_inc(s["products"], 1)
                dve.wait_ge(s["products"], n + 1)
                dve.wait_ge(s["rest"], n)
                dve.tensor_tensor(rot[:, :, :], t_cos[:, :, :], t_sin[:, :, :], ALU.add).then_inc(s["rot"], 1)
                dve.wait_ge(s["high"], n + 1)
                dve.wait_ge(s["low"], n)
                dve.tensor_tensor(rest[:, :, :], rot[:, :, :], parts[:, 0, :, :], ALU.subtract).then_inc(s["rest"], 1)
                dve.wait_ge(s["middle"], n + 1)
                dve.tensor_tensor(parts[:, 2, :, :], rest[:, :, :], parts[:, 1, :, :], ALU.subtract).then_inc(s["low"], 1)

            def act(self, act, n, b, half):
                s = self.s
                act.wait_ge(s["rot"], n + 1)
                act.wait_ge(s["stored"], n * N_STORES)
                act.activation(parts[:, 0, :, :], rot[:, :, :], ACT.Copy).then_inc(s["high"], 1)
                act.wait_ge(s["v"], n + 1)
                to = v_all[:, bass.ts(b, S)].rearrange("p (h k c) -> p k h c", h=H // HG, k=NQT)
                act.activation(to[:, half * GT:(half + 1) * GT, :, :],
                               bank[4].rearrange("p (k h c) -> p k h c", k=GT, h=H // HG), ACT.Copy).then_inc(s["v_kept"], 1)
                act.wait_ge(s["rest"], n + 1)
                act.activation(parts[:, 1, :, :], rest[:, :, :], ACT.Copy).then_inc(s["middle"], 1)

            def sp(self, sp, n, b, half):
                s, a = self.s, self.a
                for part, ready in ((0, "high"), (1, "middle"), (2, "low")):
                    sp.wait_ge(s[ready], n + 1)
                    for qk, slots in enumerate((Q_SLOTS, K_SLOTS)):
                        for slot in range(NS):
                            if slots[slot] != part:
                                continue
                            d = dram["qk"[qk] + str(a)][bass.ts(b, H // HG), :, slot * DH:(slot + 1) * DH, :]
                            d = d.rearrange("g r d (l s) -> g r (d l) s", l=2)
                            for hg in range(H // HG):
                                sp.dma_start(d[hg, :, :, half * G:(half + 1) * G],
                                             parts[hg * 32:(hg + 1) * 32, part, qk, :]).then_inc(s["stored"], 16)

        N_STORES = 2 * NS * (H // HG) * 16
        proj = {a: Project(a) for a in (1, 2)}

        class Attention:

            def __init__(self, a):
                self.a = a
                self.causal = a == 1
                self.chunks, self.steps, self.order = attention_plan(self.causal)
                self.nc, self.ns, self.nu = len(self.chunks), len(self.steps), 2 * len(self.steps)
                names = ("v_in", "chunk", "chunk_max", "maxima", "max_T", "max_out", "max_in",
                         "scores", "exps", "values", "sums", "spread", "rcp", "norm", "ready", "cleared")
                self.s = {x: sem(f"attend{a}_{x}") for x in names}
                self.rows_in = [sem(f"attend{a}_rows_in{i}") for i in range(QB)]
                self.out = [sem(f"attend{a}_out{i}") for i in range(HALVES)]

            def load(self, sp, i, buf):
                for tile, name in ((q_rows, "q"), (k_rows, "k")):
                    for par in range(2):
                        src = dram[f"{name}{self.a}"][bass.ds(i, 1), par, :, :].rearrange("o r s -> (o r) s")
                        sp.dma_start(tile[buf][64 * par:64 * par + KS, :, :].rearrange("p l s -> p (l s)"),
                                     src).then_inc(self.rows_in[buf], 16)

            def sp_maxima(self, sp, i, buf):
                sp.wait_ge(self.s["max_out"], i + 1)
                for j in range(HG):
                    pair, par = divmod(j, 2)
                    sp.dma_start(q_rows[buf][64 * par + KS:64 * par + KM, pair, :],
                                 max_T[3 * j:3 * j + 3, :]).then_inc(self.s["max_in"], 16)

            def sp(self, sp):
                sp.wait_ge(self.s["ready"], 1)
                for i in range(QB):
                    self.load(sp, i, i)
                self.sp_maxima(sp, 0, 0)

                def iteration(i, k, load):
                    self.sp_maxima(sp, i + 1, (k + 1) % QB)
                    if load:
                        sp.wait_ge(self.s["scores"], (i + 1) * self.nu)
                        self.load(sp, i + QB, k % QB)

                with sp.Fori(0, (NG - QB - 1) // QB) as r:
                    for k in range(QB):
                        iteration(QB * r + k, k, True)
                for i in range((NG - QB - 1) // QB * QB, NG - 1):
                    iteration(i, i, i + QB < NG)

            def pe(self, pe):
                s = self.s

                def chunk(g, c, buf, turn):
                    qt, pair, par, kh, width, masked = self.chunks[c]
                    if c == 0:
                        pe.wait_ge(self.rows_in[buf], 64 * (turn + 1))
                    if c >= 2 or not at_start(g):
                        pe.wait_ge(s["chunk_max"], g * self.nc + c - 1)
                    r = slice(64 * par, 64 * par + KS)
                    last = pe.matmul(bank[4 + c % 2][:, 0:width], q_rows[buf][r, pair, qt * P:(qt + 1) * P],
                                     k_rows[buf][r, pair, kh * G:kh * G + width], start=True, stop=not masked)
                    if masked:
                        last = pe.matmul(bank[4 + c % 2][:, width - P:width], ident_b[:, :], later_keys[:, :],
                                         start=False, stop=True)
                    last.then_inc(s["chunk"], 1)

                def maxima(g):
                    pe.wait_ge(s["maxima"], 5 * (g + 1))
                    if not at_start(g):
                        pe.wait_ge(s["rcp"], HALVES * g)
                    view = bank[7].bitcast(BF16)
                    for qt in range(NQT):
                        last = pe.transpose(view[0:3 * HG, qt * P:(qt + 1) * P],
                                            max_parts[:, qt, :, :].rearrange("p j c -> p (j c)"), ident_b[:, :])
                    last.then_inc(s["max_T"], 1)

                def unit(i, u, buf):
                    qh, kt, c0, masked, *_ = self.steps[u // 2]
                    pair = u % 2
                    if u == 0:
                        pe.wait_ge(s["max_in"], 64 * (i + 1))
                    if u >= 2 or not at_start(i):
                        pe.wait_ge(s["exps"], i * self.nu + u - 1)
                    for par in range(2):
                        r = slice(64 * par, 64 * par + KM)
                        last = pe.matmul(bank[2 * (u % 2) + par][:, 0:G - c0], k_rows[buf][r, pair, kt * P:(kt + 1) * P],
                                         q_rows[buf][r, pair, qh * G + c0:(qh + 1) * G], start=True, stop=not masked)
                    if masked:
                        for par in range(2):
                            last = pe.matmul(bank[2 * (u % 2) + par][:, 0:P], ident_b[:, :], later_keys_T[:, :],
                                             start=False, stop=True)
                    last.then_inc(s["scores"], 1)

                def values(i, k, buf):
                    qh, kt, c0, _, first, last_kt = self.steps[k]
                    pe.wait_ge(s["exps"], i * self.nu + 2 * k + 2)
                    if k == 0:
                        pe.wait_ge(s["v_in"], i + 1)
                    if first and (qh or not at_start(i)):
                        pe.wait_ge(s["sums"], HALVES * i + qh)
                    for j in range(HG):
                        pair, par = divmod(j, 2)
                        last = pe.matmul(bank[6][32 * j:32 * j + 32, c0:G], v_ones[buf][:, kt, j, :],
                                         probs[:, (2 * k + pair) % NRING, par, 0:G - c0], start=first, stop=last_kt)
                    last.then_inc(s["values"], 1)

                def finish(i, qh):
                    pe.wait_ge(s["sums"], HALVES * i + qh + 1)
                    if qh:
                        pe.wait_ge(s["rcp"], HALVES * i + qh)
                    else:
                        pe.wait_ge(s["max_out"], i + 1)
                    pe.matmul(bank[7], sel[:, :], o_sums[:, qh, :], start=True, stop=True).then_inc(s["spread"], 1)

                def iteration(i, k, more, r=0):
                    for what, n in self.order:
                        if what == "chunk" and more:
                            chunk(i + 1, n, (k + 1) % QB, r + (k + 1) // QB)
                        if what == "unit":
                            unit(i, n, k % QB)
                        if what == "values":
                            values(i, n, k % QB)
                        if what == "finish":
                            finish(i, n)
                    if more:
                        maxima(i + 1)

                for c in range(self.nc):
                    chunk(0, c, 0, 0)
                maxima(0)
                iteration(0, 0, True)
                with pe.Fori(0, (NG - 2) // QB) as r:
                    for k in range(QB):
                        iteration(QB * r + (k + 1), k + 1, True, r)
                for i in range((NG - 2) // QB * QB + 1, NG):
                    iteration(i, i, i + 1 < NG)

            def dve(self, dve):
                s = self.s

                def chunk(g, c):
                    qt, pair, par, kh, width, _ = self.chunks[c]
                    n = g * self.nc + c
                    if c == 0 and not at_start(g):
                        dve.wait_ge(s["maxima"], 5 * g)
                    dve.wait_ge(s["chunk"], n + 1)
                    to = row_max[:, qt, 2 * pair + par, kh:kh + 1]
                    src = bank[4 + c % 2][:, 0:width]
                    dve.tensor_reduce(to, src, AX.X, ALU.max).then_inc(s["chunk_max"], 1)

                def maxima(g):
                    dve.wait_ge(s["chunk_max"], (g + 1) * self.nc)
                    dve.tensor_reduce(top_max[:, :], row_max[:, :, :, :].rearrange("p t j h -> p (t j) h"), AX.X,
                                      ALU.max).then_inc(s["maxima"], 1)
                    dve.wait_ge(s["maxima"], 5 * g + 1)
                    if not at_start(g):
                        dve.wait_ge(s["max_T"], g)
                    part = [max_parts[:, :, :, i] for i in range(3)]
                    tm = top_max[:, :].rearrange("p (t j) -> p t j", j=HG)
                    r0 = max_rest[:, 0, :].rearrange("p (t j) -> p t j", j=HG)
                    dve.tensor_scalar(part[0], tm, -1.0, None, ALU.mult).then_inc(s["maxima"], 1)
                    dve.wait_ge(s["maxima"], 5 * g + 2)
                    dve.scalar_tensor_tensor(r0, tm, -1.0, part[0], ALU.mult, ALU.subtract).then_inc(s["maxima"], 1)
                    dve.wait_ge(s["maxima"], 5 * g + 3)
                    dve.tensor_copy(part[1], r0).then_inc(s["maxima"], 1)
                    dve.wait_ge(s["maxima"], 5 * g + 4)
                    dve.tensor_tensor(part[2], r0, part[1], ALU.subtract).then_inc(s["maxima"], 1)

                def finish(i, qh):
                    dve.wait_ge(s["spread"], HALVES * i + qh + 1)
                    if not at_start(i):
                        dve.wait_ge(s["norm"], HALVES * (i - 1) + qh + 1)
                    dve.reciprocal(o_rcp[:, qh, :], bank[7]).then_inc(s["rcp"], 1)

                def iteration(i, more):
                    for what, n in self.order:
                        if what == "chunk" and more:
                            chunk(i + 1, n)
                        if what == "finish" and (n < HALVES - 1 or not more):
                            finish(i, n)
                    if more:
                        maxima(i + 1)
                        finish(i, HALVES - 1)

                dve.memset(row_max[:, :, :, :], LOW).then_inc(s["cleared"], 1)
                dve.wait_ge(s["cleared"], 1)
                for c in range(self.nc):
                    chunk(0, c)
                maxima(0)
                iteration(0, True)
                with dve.Fori(0, (NG - 2) // QB) as r:
                    for k in range(QB):
                        iteration(QB * r + (k + 1), True)
                for i in range((NG - 2) // QB * QB + 1, NG):
                    iteration(i, i + 1 < NG)

            def act(self, act):
                s = self.s

                def maxima(g):
                    act.wait_ge(s["max_T"], g + 1)
                    if not at_start(g):
                        act.wait_ge(s["max_in"], 64 * g)
                    act.activation(max_T[:, :], bank[7].bitcast(BF16)[0:3 * HG, :], ACT.Copy).then_inc(s["max_out"], 1)

                def unit(i, u):
                    _, _, c0, *_ = self.steps[u // 2]
                    act.wait_ge(s["scores"], i * self.nu + u + 1)
                    if u >= NRING or not at_start(i):
                        act.wait_ge(s["values"], i * self.ns + (u - NRING) // 2 + 1)
                    act.activation(probs[:, u % NRING, :, 0:G - c0], banks03[:, 2 * (u % 2):2 * (u % 2) + 2, 0:G - c0],
                                   ACT.Exp, scale=SCALE).then_inc(s["exps"], 1)

                def values(i, k):
                    qh, *_, last_kt = self.steps[k]
                    if not last_kt:
                        return
                    act.wait_ge(s["values"], i * self.ns + k + 1)
                    if not at_start(i):
                        act.wait_ge(s["norm"], HALVES * (i - 1) + qh + 1)
                    act.activation(o_sums[:, qh, :], bank[6], ACT.Copy).then_inc(s["sums"], 1)

                def iteration(i, more):
                    for what, n in self.order:
                        if what == "unit":
                            unit(i, n)
                        if what == "values":
                            values(i, n)
                    if more:
                        maxima(i + 1)

                maxima(0)
                iteration(0, True)
                with act.Fori(0, (NG - 2) // QB) as r:
                    for k in range(QB):
                        iteration(QB * r + (k + 1), True)
                for i in range((NG - 2) // QB * QB + 1, NG):
                    iteration(i, i + 1 < NG)

            def pool(self, pool):
                s = self.s

                def v_in(g, buf):
                    if not at_start(g - 1) and not at_start(g):
                        pool.wait_ge(s["values"], (g - 1) * self.ns)
                    src = v_all[:, bass.ts(g, NQT * HG * DH)].rearrange("p (k j d) -> p k j d", k=NQT, j=HG)
                    pool.tensor_copy(v_ones[buf][:, :, :, 0:DH], src).then_inc(s["v_in"], 1)

                def finish(i, qh):
                    pool.wait_ge(s["rcp"], HALVES * i + qh + 1)
                    if not at_start(i):
                        pool.wait_ge(self.out[qh], 16 * i)
                    pool.tensor_tensor(o_norm[:, qh, :], o_sums[:, qh, :], o_rcp[:, qh, :], ALU.mult).then_inc(s["norm"], 1)
                    pool.wait_ge(s["norm"], HALVES * i + qh + 1)
                    d = dram[f"o{self.a}"][bass.ds(i, 1), :, qh * G:(qh + 1) * G].rearrange("o p s -> (o p) s")
                    pool.dma_start(d, o_norm[:, qh, :]).then_inc(self.out[qh], 16)

                def iteration(i, k, more):
                    if more:
                        v_in(i + 1, (k + 1) % QB)
                    for what, n in self.order:
                        if what == "finish":
                            finish(i, n)

                for i in range(QB):
                    pool.memset(k_rows[i][:, :, :], 1.0)
                    last = pool.memset(v_ones[i][:, :, :, :], 1.0)
                last.then_inc(s["ready"], 1)
                pool.wait_ge(s["ready"], 1)
                v_in(0, 0)
                iteration(0, 0, True)
                with pool.Fori(0, (NG - 2) // QB) as r:
                    for k in range(QB):
                        iteration(QB * r + (k + 1), k + 1, True)
                for i in range((NG - 2) // QB * QB + 1, NG):
                    iteration(i, i, i + 1 < NG)
                for qh in range(HALVES):
                    pool.wait_ge(self.out[qh], 16 * NG)

        at = {a: Attention(a) for a in (1, 2)}

        first = {x: sem(f"first_{x}") for x in ("x_in", "ln_out")}
        f_outer, f_inner = Norm("first_outer", 0), Norm("first_inner", 1)
        mid = {x: sem(f"mid_{x}") for x in ("in", "attended", "x2", "T", "yT", "up", "gelu", "down", "f", "x", "out")}
        m_inner, m_outer = Norm("mid_inner", 0), Norm("mid_outer", 1)
        end = {x: sem(f"end_{x}") for x in ("in", "attended", "s", "link", "x1", "T", "yT", "logits", "gap", "e2", "comb",
                                            "up", "gelu", "down", "sum", "y", "out")}
        e_first, e_last = Norm("end_first", 0), Norm("end_last", 1)

        def groups(eng):
            for half in range(HALVES):
                yield 0, half, half
            with eng.Fori(1, B) as b:
                for half in range(HALVES):
                    yield b, half, b * HALVES + half

        def transposes(pe, to, src):
            for g in range(GT):
                last = pe.transpose(to[:, g * P:(g + 1) * P], src[:, g, :], ident[:, :])
            return last

        def heads_product(pe, a):
            for g in range(GT):
                for hg in range(HG):
                    last = pe.matmul(bank[6][:, g * P:(g + 1) * P], heads_in[:, hg, g * P:(g + 1) * P], w_o[a][:, hg, :],
                                     start=(hg == 0), stop=(a == 1 and hg == HG - 1))
                if a == 2:
                    last = pe.matmul(bank[6][:, g * P:(g + 1) * P], ones_row[:, :], rows[:, 1, :], start=False, stop=True)
            return last

        def down_product(pe, to, h, w, bias):
            for g in range(GT):
                for f in range(FC):
                    pe.matmul(to[:, g * P:(g + 1) * P], hidden[:, h, f, g * P:(g + 1) * P], w[:, f, :],
                              start=(f == 0), stop=False)
                last = pe.matmul(to[:, g * P:(g + 1) * P], ones_row[:, :], bias, start=False, stop=True)
            return last

        def flat(tile):
            return tile[:, :, :].rearrange("p t d -> p (t d)")

        block = ctx.enter_context(nc.Block())

        loads = []

        def constant(to, src):
            loads.append((to, src))

        constant(ident[:, :], t["ident"])
        constant(ident_b[:, :], t["ident_b"])
        constant(sel[:, :], t["sel"])
        constant(later_keys[:, :], t["later_keys"])
        constant(later_keys_T[:, :], t["later_keys_T"])
        constant(iota_e[:, :], t["iota_e"])
        for a in (1, 2):
            constant(rope[a][:, :, :], t[f"rope{a}"])
            constant(w_qk[a][:, :, :], t[f"w_qk{a}"])
            constant(w_v[a][:, :], t[f"w_v{a}"])
            for head in range(H):
                hg, j = divmod(head, HG)
                constant(w_o[a][32 * j:32 * j + DH, hg, :], t[f"w_o{a}"][head * DH:(head + 1) * DH, :])
        constant(b_qk[:, :], t["b_qk"])
        for i, x in enumerate(("bv", "bo", "b2")):
            constant(rows[:, i, :], t[x].rearrange("(o d) -> o d", o=1))
        constant(rows[:, 4:4 + E, :], t["eb2"].rearrange("(o e) d -> o e d", o=1))
        constant(bg_row[:, :], t["bg"].rearrange("(o e) -> o e", o=1))
        for i, x in enumerate(("ln1_g", "ln1_b", "ln2_g", "ln2_b")):
            constant(cols1[:, i:i + 1], t[x].rearrange("(d o) -> d o", o=1))
        for i, x in enumerate(("g1", "be1", "g2", "be2")):
            constant(ln_rows[:, i, :], t[x].rearrange("(o d) -> o d", o=1).broadcast_to([P, D]))
        constant(w1[:, :], t["w1"])
        constant(b1c[:, :], t["b1c"])
        constant(w2[:, :, :], t["w2"].rearrange("(f p) d -> p f d", p=P))
        constant(wg[:, :], t["wg"])
        constant(ew1[:, :, :], t["ew1"].rearrange("e d f -> d e f"))
        constant(eb1[:, :, :], t["eb1c"])
        constant(ew2[:, :, :, :], t["ew2"].rearrange("e (f p) d -> p e f d", p=P))

        def ready(eng):
            eng.wait_ge(loaded, 16 * len(loads))
            eng.wait_ge(set_up, 1)

        @block.sync
        def _(sp):
            sp.wait_ge(set_up, 1)
            for to, src in loads:
                sp.dma_start(to, src).then_inc(loaded, 16)
            for b, half, n in groups(sp):
                sp.wait_ge(f_outer.done, 5 * n + 5)
                sp.dma_start(tokens(x_ln_d, b, half), xb[:, :, :]).then_inc(first["ln_out"], 16)
                proj[1].sp(sp, n, b, half)
            sp.wait_ge(first["ln_out"], 16 * B * HALVES)
            sp.wait_ge(proj[1].s["stored"], N_STORES * B * HALVES)
            barrier(sp, 1)
            at[1].sp(sp)
            barrier(sp, 2)
            for b, half, n in groups(sp):
                sp.wait_ge(mid["x"], n + 1)
                sp.dma_start(tokens(x_mid_d, b, half), xf[:, :, :]).then_inc(mid["out"], 16)
                sp.wait_ge(m_outer.done, 5 * n + 5)
                sp.dma_start(tokens(z_d, b, half), xz[:, :, :]).then_inc(mid["out"], 16)
                proj[2].sp(sp, n, b, half)
            sp.wait_ge(mid["out"], 32 * B * HALVES)
            sp.wait_ge(proj[2].s["stored"], N_STORES * B * HALVES)
            barrier(sp, 3)
            at[2].sp(sp)
            barrier(sp, 4)
            for b, half, n in groups(sp):
                sp.wait_ge(end["y"], n + 1)
                sp.dma_start(tokens(x_out, b, half), xa[:, :, :]).then_inc(end["out"], 16)
            sp.wait_ge(end["out"], 16 * B * HALVES)

        @block.gpsimd
        def _(pool):
            for a in (1, 2):
                pool.memset(w_o[a][:, :, :], 0.0)
            pool.memset(ones_row[:, :], 1.0)
            pool.memset(eps_col[:, :], EPS)
            pool.memset(e_base[:, :], float(np.exp(1.0)))
            pool.memset(minus_half[:, :], -0.5).then_inc(set_up, 1)
            ready(pool)
            for b, half, n in groups(pool):
                pool.wait_ge(f_outer.done, 5 * n)
                pool.dma_start(xt[:, :, :], tokens(x_in, b, half)).then_inc(first["x_in"], 16)
                f_outer.root(pool, n)
                f_inner.root(pool, n)
            barrier(pool, 1)
            at[1].pool(pool)
            barrier(pool, 2)
            for b, half, n in groups(pool):
                pool.wait_ge(mid["x"], n)
                pool.dma_start(heads_in[:, :, :], dram["o1"][bass.ds(b * HG, HG), :, half * G:(half + 1) * G]
                               .rearrange("g p s -> p g s")).then_inc(mid["in"], 16)
                pool.dma_start(xb[:, :, :], tokens(x_ln_d, b, half)).then_inc(mid["in"], 16)
                pool.dma_start(xt[:, :, :], tokens(x_in, b, half)).then_inc(mid["in"], 16)
                m_inner.root(pool, n)
                m_outer.root(pool, n)
            barrier(pool, 3)
            at[2].pool(pool)
            barrier(pool, 4)
            for b, half, n in groups(pool):
                pool.wait_ge(end["y"], n)
                pool.dma_start(heads_in[:, :, :], dram["o2"][bass.ds(b * HG, HG), :, half * G:(half + 1) * G]
                               .rearrange("g p s -> p g s")).then_inc(end["in"], 16)
                pool.dma_start(xb[:, :, :], tokens(z_d, b, half)).then_inc(end["in"], 16)
                pool.dma_start(xt[:, :, :], tokens(x_mid_d, b, half)).then_inc(end["in"], 16)
                e_first.root(pool, n)
                pool.wait_ge(end["gap"], n + 1)
                pool.tensor_tensor(e2[:, :], e_base[:, :], gap[:, :], ALU.pow).then_inc(end["e2"], 1)
                e_last.root(pool, n)

        @block.tensor
        def _(pe):
            ready(pe)
            for b, half, n in groups(pe):
                proj[1].pe(pe, n, xz, f_inner.done, 5 * n + 5)
            barrier(pe, 1)
            at[1].pe(pe)
            barrier(pe, 2)
            for b, half, n in groups(pe):
                pe.wait_ge(mid["in"], 48 * (n + 1))
                pe.wait_ge(mid["f"], n)
                heads_product(pe, 1).then_inc(mid["attended"], 1)
                pe.wait_ge(m_inner.done, 5 * n + 5)
                pe.wait_ge(mid["yT"], n)
                transposes(pe, bank[7], xd).then_inc(mid["T"], 1)
                pe.wait_ge(mid["yT"], n + 1)
                pe.wait_ge(proj[2].s["products"], n)
                for f in range(FC):
                    pe.matmul(bank[f], w1[:, f * P:(f + 1) * P], yT[:, :], start=True, stop=True).then_inc(mid["up"], 1)
                pe.wait_ge(mid["gelu"], FC * (n + 1))
                down_product(pe, bank[6], 0, w2, rows[:, 2, :]).then_inc(mid["down"], 1)
                proj[2].pe(pe, n, xz, m_outer.done, 5 * n + 5)
            barrier(pe, 3)
            at[2].pe(pe)
            barrier(pe, 4)
            for b, half, n in groups(pe):
                pe.wait_ge(end["in"], 48 * (n + 1))
                pe.wait_ge(end["sum"], E * n)
                heads_product(pe, 2).then_inc(end["attended"], 1)
                pe.wait_ge(end["x1"], n + 1)
                pe.wait_ge(end["yT"], n)
                transposes(pe, bank[7], xf).then_inc(end["T"], 1)
                pe.wait_ge(end["yT"], n + 1)
                for g in range(GT):
                    o = bank[5][:, g * E:(g + 1) * E]
                    pe.matmul(o, yT[:, g * P:(g + 1) * P], wg[:, :], start=True, stop=False)
                    last = pe.matmul(o, ones_row[:, :], bg_row[:, :], start=False, stop=True)
                last.then_inc(end["logits"], 1)

                def up(e):
                    for f in range(FC):
                        if e:
                            pe.wait_ge(end["gelu"], FC * (E * n + e - 1) + f + 1)
                        pe.matmul(bank[f], ew1[:, e, f * P:(f + 1) * P], yT[:, :], start=True,
                                  stop=True).then_inc(end["up"], 1)

                up(0)
                for e in range(E):
                    if e + 1 < E:
                        up(e + 1)
                    pe.wait_ge(end["gelu"], FC * (E * n + e + 1))
                    if e >= 2:
                        pe.wait_ge(end["sum"], E * n + e - 1)
                    down_product(pe, bank[4 + 2 * (e % 2)], e % 2, ew2[:, e, :, :],
                                 rows[:, 4 + e, :]).then_inc(end["down"], 1)

        @block.vector
        def _(dve):
            ready(dve)
            for b, half, n in groups(dve):
                dve.wait_ge(first["x_in"], 16 * (n + 1))
                f_outer.statistics(dve, n, xt)
                dve.wait_ge(first["ln_out"], 16 * n)
                f_outer.apply(dve, n, xb, xt)
                dve.wait_ge(f_outer.done, 5 * n + 5)
                f_inner.statistics(dve, n, xb)
                dve.wait_ge(proj[1].s["zT"], n)
                f_inner.apply(dve, n, xz, xb)
                proj[1].dve(dve, n, half)
            barrier(dve, 1)
            at[1].dve(dve)
            barrier(dve, 2)
            for b, half, n in groups(dve):
                dve.wait_ge(mid["in"], 48 * (n + 1))
                dve.wait_ge(mid["attended"], n + 1)
                dve.tensor_tensor(flat(xc), bank[6], flat(xb), ALU.add).then_inc(mid["x2"], 1)
                dve.wait_ge(mid["x2"], n + 1)
                m_inner.statistics(dve, n, xc)
                m_inner.apply(dve, n, xd, xc)
                dve.wait_ge(mid["T"], n + 1)
                dve.tensor_scalar(yT[:, :], bank[7], cols1[:, 2:3], cols1[:, 3:4], ALU.mult, ALU.add).then_inc(mid["yT"], 1)
                dve.wait_ge(mid["down"], n + 1)
                dve.tensor_tensor(flat(xe), bank[6], flat(xc), ALU.add).then_inc(mid["f"], 1)
                dve.wait_ge(mid["f"], n + 1)
                dve.wait_ge(mid["out"], 32 * n)
                dve.tensor_tensor(flat(xf), flat(xe), flat(xt), ALU.add).then_inc(mid["x"], 1)
                dve.wait_ge(mid["x"], n + 1)
                m_outer.statistics(dve, n, xf)
                dve.wait_ge(proj[2].s["zT"], n)
                m_outer.apply(dve, n, xz, xf)
                proj[2].dve(dve, n, half)
            barrier(dve, 3)
            at[2].dve(dve)
            barrier(dve, 4)
            LINKS = 13
            for b, half, n in groups(dve):
                links = [0]

                def link(ins):
                    links[0] += 1
                    ins.then_inc(end["link"], 1)
                    dve.wait_ge(end["link"], LINKS * n + links[0])

                def rows_of(i):
                    return ln_rows[:, i:i + 1, :].broadcast_to([P, GT, D])

                dve.wait_ge(end["in"], 48 * (n + 1))
                dve.wait_ge(end["attended"], n + 1)
                link(dve.tensor_tensor(flat(xc), bank[6], flat(xb), ALU.add))
                e_first.statistics(dve, n, xc)
                e_first.apply(dve, n, xd, xc)
                dve.wait_ge(e_first.done, 5 * n + 5)
                link(dve.tensor_tensor(xe[:, :, :], xd[:, :, :], rows_of(0), ALU.mult))
                dve.wait_ge(end["T"], n)
                dve.tensor_tensor(xf[:, :, :], xe[:, :, :], rows_of(1), ALU.add).then_inc(end["x1"], 1)
                dve.wait_ge(end["T"], n + 1)
                dve.wait_ge(end["up"], E * FC * n)
                dve.tensor_copy(yT[:, :], bank[7]).then_inc(end["yT"], 1)
                dve.wait_ge(end["logits"], n + 1)
                link(dve.tensor_copy(gate[:, :, :].rearrange("p t e -> p (t e)"), bank[5][:, 0:GT * E]))
                carry_wait(dve)
                for g in range(GT):
                    last = dve.max(top[:, g, :], gate[:, g, :])
                link(last)
                carry_wait(dve)
                for g in range(GT):
                    last = dve.max_index(top_i[:, g, :], top[:, g, :], gate[:, g, :])
                link(last)
                dve.tensor_tensor(gap[:, :], top[:, :, 1], top[:, :, 0], ALU.subtract).then_inc(end["gap"], 1)
                link(dve.tensor_copy(top_f[:, :, :], top_i[:, :, 0:2]))
                dve.wait_ge(end["e2"], n + 1)
                link(dve.tensor_scalar(esum[:, :], e2[:, :], 1.0, 0.0, ALU.add, ALU.add))
                link(dve.reciprocal(pw[:, :, 0], esum[:, :]))
                link(dve.tensor_tensor(pw[:, :, 1], e2[:, :], pw[:, :, 0], ALU.mult))
                for g in range(GT):
                    for i in range(2):
                        last = dve.tensor_scalar(comb[:, i, g, :], iota_e[:, :], top_f[:, g, i:i + 1], pw[:, g, i:i + 1],
                                                 ALU.is_equal, ALU.mult)
                link(last)
                link(dve.tensor_tensor(comb[:, 0, :, :], comb[:, 0, :, :], comb[:, 1, :, :], ALU.add))
                dve.wait_ge(end["out"], 16 * n)
                for e in range(E):
                    dve.wait_ge(end["down"], E * n + e + 1)
                    if e:
                        dve.wait_ge(end["sum"], E * n + e)
                    for g in range(GT):
                        last = dve.scalar_tensor_tensor(xa[:, g, :], bank[4 + 2 * (e % 2)][:, g * P:(g + 1) * P],
                                                        comb[:, 0, g, e:e + 1], (xa if e else xf)[:, g, :], ALU.mult, ALU.add)
                    last.then_inc(end["sum"], 1)
                dve.wait_ge(end["sum"], E * (n + 1))
                e_last.statistics(dve, n, xa)
                e_last.apply(dve, n, xz, xa)
                dve.wait_ge(e_last.done, 5 * n + 5)
                link(dve.tensor_tensor(xc[:, :, :], xz[:, :, :], rows_of(2), ALU.mult))
                link(dve.tensor_tensor(xe[:, :, :], xc[:, :, :], rows_of(3), ALU.add))
                assert links[0] == LINKS
                dve.tensor_tensor(flat(xa), flat(xe), flat(xt), ALU.add).then_inc(end["y"], 1)

        @block.scalar
        def _(act):
            ready(act)
            for b, half, n in groups(act):
                proj[1].act(act, n, b, half)
            barrier(act, 1)
            at[1].act(act)
            barrier(act, 2)
            for b, half, n in groups(act):
                for f in range(FC):
                    act.wait_ge(mid["up"], FC * n + f + 1)
                    act.wait_ge(mid["down"], n)
                    act.activation(hidden[:, 0, f, :], bank[f], ACT.Gelu, bias=b1c[:, f:f + 1]).then_inc(mid["gelu"], 1)
                proj[2].act(act, n, b, half)
            barrier(act, 3)
            at[2].act(act)
            barrier(act, 4)
            for b, half, n in groups(act):
                for e in range(E):
                    for f in range(FC):
                        act.wait_ge(end["up"], FC * (E * n + e) + f + 1)
                        if e >= 2:
                            act.wait_ge(end["down"], E * n + e - 1)
                        else:
                            act.wait_ge(end["down"], E * n)
                        act.activation(hidden[:, e % 2, f, :], bank[f], ACT.Gelu,
                                       bias=eb1[:, e, f:f + 1]).then_inc(end["gelu"], 1)


def _rope_tables(half_split):
    inv = (np.float32(10000.0) ** (-(np.arange(0, DH, 2, dtype=np.float32) / np.float32(DH)))).astype(np.float32)
    theta = np.arange(S, dtype=np.float32)[:, None] * inv[None, :]
    table = np.zeros((P, 2, S), np.float32)
    for r in range(P):
        d = r % 32 % 16 // 2
        angle, negative = (d % (DH // 2), d < DH // 2) if half_split else (d // 2, d % 2 == 0)
        table[r, 0] = np.cos(theta[:, angle])
        table[r, 1] = np.sin(theta[:, angle]) * np.float32(-1 if negative else 1)
    return table


def _columns(half_split):
    own, partner = [], []
    for r in range(P):
        hg, par, d, pair = r // 32, r % 32 // 16, r % 16 // 2, r % 2
        head = hg * HG + pair * 2 + par
        own.append(head * DH + d)
        partner.append(head * DH + ((d + DH // 2) % DH if half_split else d ^ 1))
    return own, partner


def kernel(**inputs):
    import concourse.bacc as bacc
    from concourse.bass_utils import run_bass_kernel_spmd

    a = {k.replace("L0_", ""): np.asarray(v) for k, v in inputs.items()}
    bf = mybir.dt.np(BF16)
    heads = np.arange(P)
    sel = ((heads[:, None] // 32 == heads[None, :] // 32) & (heads[:, None] % 32 == DH)).astype(np.float32)
    later = np.where(heads[None, :] > heads[:, None], LOW, 0.0)
    arrays = {
        "x": a["attn_x"],
        "ident": np.eye(P, dtype=np.float32), "ident_b": np.eye(P).astype(bf), "sel": sel,
        "later_keys": later.astype(bf), "later_keys_T": later.T.astype(bf),
        "iota_e": np.tile(np.arange(E, dtype=np.float32), (P, 1)),
        "rope1": _rope_tables(False), "rope2": _rope_tables(True),
    }
    own, partner = _columns(False)
    q, k, v = (a["attn_Wqkv"][:, i * D:(i + 1) * D] for i in range(3))
    arrays["w_qk1"] = np.stack([q[:, own], q[:, partner], k[:, own], k[:, partner]], axis=1)
    arrays["w_v1"] = v
    own, partner = _columns(True)
    q, k = a["ffn_Wq"], a["ffn_Wk"]
    arrays["w_qk2"] = np.stack([q[:, own], q[:, partner], k[:, own], k[:, partner]], axis=1)
    q, k = a["ffn_bq"], a["ffn_bk"]
    arrays["b_qk"] = np.stack([q[own], q[partner], k[own], k[partner]], axis=1)
    arrays["w_v2"] = a["ffn_Wv"]
    arrays["w_o1"], arrays["w_o2"] = a["attn_Wo"], a["ffn_Wo"]
    for x in ("ln1_g", "ln1_b", "ln2_g", "ln2_b"):
        arrays[x] = a["attn_" + x]
    for x, y in (("bv", "bv"), ("bo", "bo"), ("bg", "bg"), ("wg", "Wg"), ("g1", "g1"), ("be1", "be1"), ("g2", "g2"),
                 ("be2", "be2"), ("ew1", "W1"), ("ew2", "W2"), ("eb2", "b2")):
        arrays[x] = a["ffn_" + y]
    arrays["w1"], arrays["w2"], arrays["b2"] = a["attn_W1"], a["attn_W2"], a["attn_b2"]
    arrays["b1c"] = a["attn_b1"].reshape(FC, P).T
    arrays["eb1c"] = a["ffn_b1"].reshape(E, FC, P).transpose(2, 0, 1)
    arrays = {f"in_{k}": np.ascontiguousarray(v) for k, v in arrays.items()}

    nc = bacc.Bacc("TRN2", target_bir_lowering=False, num_devices=1)
    t = {k[3:]: nc.dram_tensor(k, v.shape, mybir.dt.from_np(v.dtype), kind="ExternalInput").ap() for k, v in arrays.items()}
    out = nc.dram_tensor("out_x", (B, S, D), F32, kind="ExternalOutput").ap()
    build(nc, t, out)
    return run_bass_kernel_spmd(nc, [arrays], core_ids=[0]).results[0]["out_x"]
```

```python
from contextlib import ExitStack

import numpy as np

import concourse.bass as bass
from concourse import mybir

F32 = mybir.dt.float32
BF16 = mybir.dt.bfloat16
U32 = mybir.dt.uint32
ALU = mybir.AluOpType
ACT = mybir.ActivationFunctionType
AX = mybir.AxisListType

P = 128
B, S, D = 4, 1024, 128
H, DH = 16, 8
E, FF = 8, 512
FC = FF // P
HG = 4
NG = B * H // HG
NQT = S // P
G = 512
GT = G // P
HALVES = S // G
T = B * S
EPS = 1e-5
SCALE = float(DH) ** -0.5
LOW = -3.0e38
Q_SLOTS = (0, 0, 1, 1, 0, 2)
K_SLOTS = (0, 1, 0, 1, 2, 0)
NS = len(Q_SLOTS)
KS = NS * DH
M0 = 2 * KS
NRING = 8
QB = 3


def at_start(i):
    return isinstance(i, int) and i == 0


def attention_plan(causal):
    chunks = []
    for qt in range(NQT):
        for kh in range(HALVES):
            width = min(G, (qt + 1) * P - kh * G) if causal else G
            if width <= 0:
                continue
            masked = causal and kh == qt // GT
            for pair in range(2):
                for par in range(2):
                    chunks.append((qt, pair, par, kh, width, masked))
    steps = []
    for qh in range(HALVES):
        n = (qh + 1) * GT if causal else NQT
        for kt in range(n):
            diagonal = causal and kt >= qh * GT
            steps.append((qh, kt, (kt - qh * GT) * P if diagonal else 0, diagonal, kt == 0, kt == n - 1))
    order, c = [], 0
    lead = 8

    def some(upto):
        nonlocal c
        while c < min(upto, len(chunks)):
            order.append(("chunk", c))
            c += 1

    some(lead)
    for k, step in enumerate(steps):
        for pair in range(2):
            order.append(("unit", 2 * k + pair))
            some(lead + (2 * k + pair + 1) * (len(chunks) - lead) // (2 * len(steps)))
        if k:
            order.append(("values", k - 1))
    some(len(chunks))
    order.append(("values", len(steps) - 1))
    return chunks, steps, order


def build(nc, t, out):
    with ExitStack() as ctx:
        def sb(name, shape, dt=F32):
            return ctx.enter_context(nc.sbuf_tensor(name, shape, dt))

        def sem(name):
            return ctx.enter_context(nc.semaphore(name))

        dram = {}
        for n in (1, 2):
            for qk in "qk":
                dram[f"{qk}{n}"] = nc.dram_tensor(f"{qk}_slots{n}", [NG, 2, NS * DH, 2 * S], BF16, kind="Internal").ap()
            dram[f"o{n}"] = nc.dram_tensor(f"heads_out{n}", [NG, P, S], F32, kind="Internal").ap()
        x_ln_d = nc.dram_tensor("x_ln_d", [T, D], F32, kind="Internal").ap()
        x_mid_d = nc.dram_tensor("x_mid_d", [T, D], F32, kind="Internal").ap()
        z_d = nc.dram_tensor("z_d", [T, D], F32, kind="Internal").ap()
        x_in = t["x"].rearrange("b s d -> (b s) d")
        x_out = out.rearrange("b s d -> (b s) d")

        def tokens(dram_ap, b, half):
            return dram_ap[bass.ds(b * S + half * G, G), :].rearrange("(t p) d -> p t d", p=P)

        ident = sb("ident", [P, P])
        ident_b = sb("ident_b", [P, P], BF16)
        later_keys = sb("later_keys", [P, P], BF16)
        later_keys_T = sb("later_keys_T", [P, P], BF16)
        rope = {n: sb(f"rope{n}", [P, 2, S]) for n in (1, 2)}
        w_qk = {n: sb(f"w_qk{n}", [P, 4, P]) for n in (1, 2)}
        w_v = {n: sb(f"w_v{n}", [P, P]) for n in (1, 2)}
        w_o = {n: sb(f"w_o{n}", [P, P]) for n in (1, 2)}
        b_qk = sb("b_qk", [P, 4])
        rows = sb("rows", [1, 4 + E, P])
        bg_row = sb("bg_row", [1, E])
        cols1 = sb("cols1", [P, 4])
        ln_rows = sb("ln_rows", [P, 4, P])
        w1 = sb("w1", [P, FF])
        b1c = sb("b1c", [P, FC])
        w2 = sb("w2", [P, FC, P])
        wg = sb("wg", [P, E])
        ew1 = sb("ew1", [P, E, FF])
        eb1 = sb("eb1", [P, E, FC])
        ew2 = sb("ew2", [P, E, FC, P])
        ones_row = sb("ones_row", [1, P])
        minus_half = sb("minus_half", [P, GT])
        e_base = sb("e_base", [P, GT])
        eps_col = sb("eps_col", [P, GT])
        carrier = sb("carrier", [P, 1])
        iota_e = sb("iota_e", [P, E])

        heads_in = sb("heads_in", [P, HG, G])
        heads_tok = sb("heads_tok", [P, GT, D])
        sums_rcp = sb("sums_rcp", [P, GT, H])
        headsT = sb("headsT", [P, G])
        yT = sb("yT", [P, G])
        hT = sb("hT", [P, G])
        stats = sb("stats", [P, 2, GT, 6])
        mv = sb("mv", [P, 2, GT, 2])
        ve = sb("ve", [P, 2, GT])
        rstd = sb("rstd", [P, 2, GT])
        parts = sb("parts", [P, 3, 2, G], BF16)
        v_all = sb("v_all", [P, NG * NQT * HG * DH])
        gate = sb("gate", [P, GT, E])
        top = sb("top", [P, GT, 8])
        top_i = sb("top_i", [P, GT, 8], U32)
        top_f = sb("top_f", [P, GT, 2])
        gap = sb("gap", [P, GT])
        e2 = sb("e2", [P, GT])
        esum = sb("esum", [P, GT])
        pw = sb("pw", [P, GT, 2])
        comb = sb("comb", [P, 2, GT, E])

        rows_work = sb("rows_work", [P, 3 * QB, 2 * S], BF16)
        k_rows = [rows_work[:, i, :].rearrange("p (l s) -> p l s", l=2) for i in range(QB)]
        q_rows = [[rows_work[:, QB + 2 * i + par, :].rearrange("p (l s) -> p l s", l=2) for par in range(2)]
                  for i in range(QB)]
        xt, xb, xc, xd, xe, xf, xz, xa = (
            rows_work[:, i, :].bitcast(F32)[:, 0:G].rearrange("p (t d) -> p t d", t=GT) for i in range(8))
        v_ones = [sb(f"v_ones{i}", [P, NQT, HG, 32]) for i in range(QB)]
        probs = sb("probs", [P, NRING, 2, G])
        hidden = probs[:, :, 0, :].rearrange("p (h f) s -> p h f s", h=2)
        t_cos, t_sin, rot, rest = (probs[:, 2 * i:2 * i + 2, 1, :] for i in range(4))
        row_max = sb("row_max", [P, NQT, HG, HALVES])
        top_max = sb("top_max", [P, NQT * HG])
        max_rest = sb("max_rest", [P, 2, NQT * HG])
        max_parts = sb("max_parts", [P, NQT, HG, 3], BF16)
        max_T = sb("max_T", [HG * 3, S], BF16)
        o_sums = sb("o_sums", [P, HALVES, G])

        banks03 = ctx.enter_context(nc.psum_tensor("banks03", [P, 4, G], F32))
        bank = [banks03[:, i, :] for i in range(4)]
        bank += [ctx.enter_context(nc.psum_tensor(f"bank{i}", [P, G], F32))[:, :] for i in range(4, 8)]

        loaded = sem("loaded")
        set_up = sem("set_up")
        phase = sem("phase")

        def barrier(eng, n):
            eng.drain().then_inc(phase, 1)
            eng.wait_ge(phase, 5 * n)

        def carry_wait(dve):
            dve.memset(carrier[:, :], 0.0)

        class Norm:

            def __init__(self, name, slot):
                self.done = sem(name)
                self.slot = slot

            def statistics(self, dve, n, src):
                i = self.slot
                if n is not None:
                    dve.wait_ge(self.done, 5 * n)
                for g in range(GT):
                    last = dve.bn_stats(stats[:, i, g, :], src[:, g, :])
                last.then_inc(self.done, 1)
                dve.wait_ge(self.done, 5 * n + 1)
                carry_wait(dve)
                for g in range(GT):
                    last = dve.bn_aggr(mv[:, i, g, :], stats[:, i, g, :])
                last.then_inc(self.done, 1)

            def root(self, pool, n):
                i = self.slot
                pool.wait_ge(self.done, 5 * n + 2)
                pool.tensor_tensor(ve[:, i, :], mv[:, i, :, 1], eps_col[:, :], ALU.add).then_inc(self.done, 1)
                pool.wait_ge(self.done, 5 * n + 3)
                pool.tensor_tensor(rstd[:, i, :], ve[:, i, :], minus_half[:, :], ALU.pow).then_inc(self.done, 1)

            def apply(self, dve, n, dst, src):
                i = self.slot
                dve.wait_ge(self.done, 5 * n + 4)
                for g in range(GT):
                    last = dve.tensor_scalar(dst[:, g, :], src[:, g, :], mv[:, i, g, 0:1], rstd[:, i, g:g + 1],
                                             ALU.subtract, ALU.mult)
                last.then_inc(self.done, 1)

        class Project:

            def __init__(self, a):
                self.a = a
                names = ("zT", "hT", "qk", "v", "v_kept", "products", "rot", "high", "rest", "middle", "low", "stored")
                self.s = {x: sem(f"project{a}_{x}") for x in names}

            def pe(self, pe, n, z, z_sem, z_value):
                s, a = self.s, self.a
                pe.wait_ge(z_sem, z_value)
                pe.wait_ge(s["hT"], n)
                for g in range(GT):
                    last = pe.transpose(bank[5][:, g * P:(g + 1) * P], z[:, g, :], ident[:, :])
                last.then_inc(s["zT"], 1)
                pe.wait_ge(s["hT"], n + 1)
                pe.wait_ge(s["products"], n)
                for i in range(4):
                    last = pe.matmul(bank[i], w_qk[a][:, i, :], hT[:, :], start=True, stop=True)
                last.then_inc(s["qk"], 1)
                pe.wait_ge(s["v_kept"], n)
                for g in range(GT):
                    o = bank[4][:, g * P:(g + 1) * P]
                    last = pe.matmul(o, hT[:, g * P:(g + 1) * P], w_v[a][:, :], start=True, stop=(a == 1))
                    if a == 2:
                        last = pe.matmul(o, ones_row[:, :], rows[:, 0, :], start=False, stop=True)
                last.then_inc(s["v"], 1)

            def dve(self, dve, n, half):
                s, a = self.s, self.a
                dve.wait_ge(s["zT"], n + 1)
                dve.wait_ge(s["v"], n)
                if a == 1:
                    dve.tensor_scalar(hT[:, :], bank[5], cols1[:, 0:1], cols1[:, 1:2], ALU.mult, ALU.add).then_inc(s["hT"], 1)
                else:
                    dve.tensor_copy(hT[:, :], bank[5]).then_inc(s["hT"], 1)
                dve.wait_ge(s["qk"], n + 1)
                dve.wait_ge(s["rot"], n)
                for i in range(4):
                    to = (t_cos, t_sin)[i % 2][:, i // 2, :]
                    table = rope[a][:, i % 2, half * G:(half + 1) * G]
                    if a == 1:
                        last = dve.tensor_tensor(to, bank[i], table, ALU.mult)
                    else:
                        last = dve.scalar_tensor_tensor(to, bank[i], b_qk[:, i:i + 1], table, ALU.add, ALU.mult)
                last.then_inc(s["products"], 1)
                dve.wait_ge(s["products"], n + 1)
                dve.wait_ge(s["rest"], n)
                dve.tensor_tensor(rot[:, :, :], t_cos[:, :, :], t_sin[:, :, :], ALU.add).then_inc(s["rot"], 1)
                dve.wait_ge(s["high"], n + 1)
                dve.wait_ge(s["low"], n)
                dve.tensor_tensor(rest[:, :, :], rot[:, :, :], parts[:, 0, :, :], ALU.subtract).then_inc(s["rest"], 1)
                dve.wait_ge(s["middle"], n + 1)
                dve.tensor_tensor(parts[:, 2, :, :], rest[:, :, :], parts[:, 1, :, :], ALU.subtract).then_inc(s["low"], 1)

            def act(self, act, n, b, half):
                s = self.s
                act.wait_ge(s["rot"], n + 1)
                act.wait_ge(s["stored"], n * N_STORES)
                act.activation(parts[:, 0, :, :], rot[:, :, :], ACT.Copy).then_inc(s["high"], 1)
                act.wait_ge(s["v"], n + 1)
                to = v_all[:, bass.ts(b, S)].rearrange("p (h k c) -> p k h c", h=H // HG, k=NQT)
                act.activation(to[:, half * GT:(half + 1) * GT, :, :],
                               bank[4].rearrange("p (k h c) -> p k h c", k=GT, h=H // HG), ACT.Copy).then_inc(s["v_kept"], 1)
                act.wait_ge(s["rest"], n + 1)
                act.activation(parts[:, 1, :, :], rest[:, :, :], ACT.Copy).then_inc(s["middle"], 1)

            def sp(self, sp, n, b, half):
                s, a = self.s, self.a
                for part, ready in ((0, "high"), (1, "middle"), (2, "low")):
                    sp.wait_ge(s[ready], n + 1)
                    for qk, slots in enumerate((Q_SLOTS, K_SLOTS)):
                        for slot in range(NS):
                            if slots[slot] != part:
                                continue
                            d = dram["qk"[qk] + str(a)][bass.ts(b, H // HG), :, slot * DH:(slot + 1) * DH, :]
                            d = d.rearrange("g r d (l s) -> g r (d l) s", l=2)
                            for hg in range(H // HG):
                                sp.dma_start(d[hg, :, :, half * G:(half + 1) * G],
                                             parts[hg * 32:(hg + 1) * 32, part, qk, :]).then_inc(s["stored"], 16)

        N_STORES = 2 * NS * (H // HG) * 16
        proj = {a: Project(a) for a in (1, 2)}

        class Attention:

            def __init__(self, a):
                self.a = a
                self.causal = a == 1
                self.chunks, self.steps, self.order = attention_plan(self.causal)
                self.nc, self.ns, self.nu = len(self.chunks), len(self.steps), 2 * len(self.steps)
                names = ("v_in", "chunk", "chunk_max", "maxima", "max_T", "max_out", "max_in",
                         "scores", "exps", "values", "sums", "ready", "cleared")
                self.s = {x: sem(f"attend{a}_{x}") for x in names}
                self.rows_in = [sem(f"attend{a}_rows_in{i}") for i in range(QB)]
                self.out = [sem(f"attend{a}_out{i}") for i in range(HALVES)]

            def load(self, sp, i, buf):
                for tile, name in ((q_rows, "q"), (k_rows, "k")):
                    for par in range(2):
                        src = dram[f"{name}{self.a}"][bass.ds(i, 1), par, :, :].rearrange("o r s -> (o r) s")
                        to = tile[buf] if name == "k" else tile[buf][par]
                        sp.dma_start(to[par * KS:(par + 1) * KS, :, :].rearrange("p l s -> p (l s)"), src).then_inc(self.rows_in[buf], 16)

            def sp_maxima(self, sp, i, buf):
                sp.wait_ge(self.s["max_out"], i + 1)
                for j in range(HG):
                    pair, par = divmod(j, 2)
                    sp.dma_start(q_rows[buf][par][M0:M0 + 3, pair, :],
                                 max_T[3 * j:3 * j + 3, :]).then_inc(self.s["max_in"], 16)

            def sp(self, sp):
                sp.wait_ge(self.s["ready"], 1)
                for i in range(QB):
                    self.load(sp, i, i)
                self.sp_maxima(sp, 0, 0)

                def iteration(i, k, load):
                    self.sp_maxima(sp, i + 1, (k + 1) % QB)
                    if load:
                        sp.wait_ge(self.s["scores"], (i + 1) * self.nu)
                        self.load(sp, i + QB, k % QB)

                with sp.Fori(0, (NG - QB - 1) // QB) as r:
                    for k in range(QB):
                        iteration(QB * r + k, k, True)
                for i in range((NG - QB - 1) // QB * QB, NG - 1):
                    iteration(i, i, i + QB < NG)

            def pe(self, pe):
                s = self.s

                def chunk(g, c, buf, turn):
                    qt, pair, par, kh, width, masked = self.chunks[c]
                    if c == 0:
                        pe.wait_ge(self.rows_in[buf], 64 * (turn + 1))
                    if c >= 2 or not at_start(g):
                        pe.wait_ge(s["chunk_max"], g * self.nc + c - 1)
                    last = pe.matmul(bank[4 + c % 2][:, 0:width], q_rows[buf][par][0:M0, pair, qt * P:(qt + 1) * P],
                                     k_rows[buf][0:M0, pair, kh * G:kh * G + width], start=True, stop=not masked)
                    if masked:
                        last = pe.matmul(bank[4 + c % 2][:, width - P:width], ident_b[:, :], later_keys[:, :],
                                         start=False, stop=True)
                    last.then_inc(s["chunk"], 1)

                def maxima(g):
                    pe.wait_ge(s["maxima"], 5 * (g + 1))
                    if not at_start(g):
                        pe.wait_ge(s["max_out"], g)
                    view = bank[7].bitcast(BF16)
                    for qt in range(NQT):
                        last = pe.transpose(view[0:3 * HG, qt * P:(qt + 1) * P],
                                            max_parts[:, qt, :, :].rearrange("p j c -> p (j c)"), ident_b[:, :])
                    last.then_inc(s["max_T"], 1)

                def unit(i, u, buf):
                    qh, kt, c0, masked, *_ = self.steps[u // 2]
                    pair = u % 2
                    if u == 0:
                        pe.wait_ge(s["max_in"], 64 * (i + 1))
                    if u >= 2 or not at_start(i):
                        pe.wait_ge(s["exps"], i * self.nu + u - 1)
                    for par in range(2):
                        last = pe.matmul(bank[2 * (u % 2) + par][:, 0:G - c0], k_rows[buf][:, pair, kt * P:(kt + 1) * P],
                                         q_rows[buf][par][:, pair, qh * G + c0:(qh + 1) * G], start=True, stop=not masked)
                    if masked:
                        for par in range(2):
                            last = pe.matmul(bank[2 * (u % 2) + par][:, 0:P], ident_b[:, :], later_keys_T[:, :],
                                             start=False, stop=True)
                    last.then_inc(s["scores"], 1)

                def values(i, k, buf):
                    qh, kt, c0, _, first, last_kt = self.steps[k]
                    pe.wait_ge(s["exps"], i * self.nu + 2 * k + 2)
                    if k == 0:
                        pe.wait_ge(s["v_in"], i + 1)
                    if first and (qh or not at_start(i)):
                        pe.wait_ge(s["sums"], HALVES * i + qh)
                    for j in range(HG):
                        pair, par = divmod(j, 2)
                        last = pe.matmul(bank[6][32 * j:32 * j + 32, c0:G], v_ones[buf][:, kt, j, :],
                                         probs[:, (2 * k + pair) % NRING, par, 0:G - c0], start=first, stop=last_kt)
                    last.then_inc(s["values"], 1)

                def iteration(i, k, more, r=0):
                    for what, n in self.order:
                        if what == "chunk" and more:
                            chunk(i + 1, n, (k + 1) % QB, r + (k + 1) // QB)
                        if what == "unit":
                            unit(i, n, k % QB)
                        if what == "values":
                            values(i, n, k % QB)
                    if more:
                        maxima(i + 1)

                for c in range(self.nc):
                    chunk(0, c, 0, 0)
                maxima(0)
                iteration(0, 0, True)
                with pe.Fori(0, (NG - 2) // QB) as r:
                    for k in range(QB):
                        iteration(QB * r + (k + 1), k + 1, True, r)
                for i in range((NG - 2) // QB * QB + 1, NG):
                    iteration(i, i, i + 1 < NG)

            def dve(self, dve):
                s = self.s

                def chunk(g, c):
                    qt, pair, par, kh, width, _ = self.chunks[c]
                    n = g * self.nc + c
                    if c == 0 and not at_start(g):
                        dve.wait_ge(s["maxima"], 5 * g)
                    dve.wait_ge(s["chunk"], n + 1)
                    to = row_max[:, qt, 2 * pair + par, kh:kh + 1]
                    src = bank[4 + c % 2][:, 0:width]
                    dve.tensor_reduce(to, src, AX.X, ALU.max).then_inc(s["chunk_max"], 1)

                def maxima(g):
                    dve.wait_ge(s["chunk_max"], (g + 1) * self.nc)
                    dve.tensor_reduce(top_max[:, :], row_max[:, :, :, :].rearrange("p t j h -> p (t j) h"), AX.X,
                                      ALU.max).then_inc(s["maxima"], 1)
                    dve.wait_ge(s["maxima"], 5 * g + 1)
                    if not at_start(g):
                        dve.wait_ge(s["max_T"], g)
                    part = [max_parts[:, :, :, i] for i in range(3)]
                    tm = top_max[:, :].rearrange("p (t j) -> p t j", j=HG)
                    r0 = max_rest[:, 0, :].rearrange("p (t j) -> p t j", j=HG)
                    dve.tensor_scalar(part[0], tm, -1.0, None, ALU.mult).then_inc(s["maxima"], 1)
                    dve.wait_ge(s["maxima"], 5 * g + 2)
                    dve.scalar_tensor_tensor(r0, tm, -1.0, part[0], ALU.mult, ALU.subtract).then_inc(s["maxima"], 1)
                    dve.wait_ge(s["maxima"], 5 * g + 3)
                    dve.tensor_copy(part[1], r0).then_inc(s["maxima"], 1)
                    dve.wait_ge(s["maxima"], 5 * g + 4)
                    dve.tensor_tensor(part[2], r0, part[1], ALU.subtract).then_inc(s["maxima"], 1)

                def iteration(i):
                    for what, n in self.order:
                        if what == "chunk":
                            chunk(i + 1, n)
                    maxima(i + 1)

                dve.memset(row_max[:, :, :, :], LOW).then_inc(s["cleared"], 1)
                dve.wait_ge(s["cleared"], 1)
                for c in range(self.nc):
                    chunk(0, c)
                maxima(0)
                iteration(0)
                with dve.Fori(0, (NG - 2) // QB) as r:
                    for k in range(QB):
                        iteration(QB * r + (k + 1))
                for i in range((NG - 2) // QB * QB + 1, NG - 1):
                    iteration(i)

            def act(self, act):
                s = self.s

                def maxima(g):
                    act.wait_ge(s["max_T"], g + 1)
                    if not at_start(g):
                        act.wait_ge(s["max_in"], 64 * g)
                    act.activation(max_T[:, :], bank[7].bitcast(BF16)[0:3 * HG, :], ACT.Copy).then_inc(s["max_out"], 1)

                def unit(i, u):
                    _, _, c0, *_ = self.steps[u // 2]
                    act.wait_ge(s["scores"], i * self.nu + u + 1)
                    if u >= NRING or not at_start(i):
                        act.wait_ge(s["values"], i * self.ns + (u - NRING) // 2 + 1)
                    act.activation(probs[:, u % NRING, :, 0:G - c0], banks03[:, 2 * (u % 2):2 * (u % 2) + 2, 0:G - c0],
                                   ACT.Exp, scale=SCALE).then_inc(s["exps"], 1)

                def values(i, k):
                    qh, *_, last_kt = self.steps[k]
                    if not last_kt:
                        return
                    act.wait_ge(s["values"], i * self.ns + k + 1)
                    if not at_start(i):
                        act.wait_ge(self.out[qh], 16 * i)
                    act.activation(o_sums[:, qh, :], bank[6], ACT.Copy).then_inc(s["sums"], 1)

                def iteration(i, more):
                    for what, n in self.order:
                        if what == "unit":
                            unit(i, n)
                        if what == "values":
                            values(i, n)
                    if more:
                        maxima(i + 1)

                maxima(0)
                iteration(0, True)
                with act.Fori(0, (NG - 2) // QB) as r:
                    for k in range(QB):
                        iteration(QB * r + (k + 1), True)
                for i in range((NG - 2) // QB * QB + 1, NG):
                    iteration(i, i + 1 < NG)

            def pool(self, pool):
                s = self.s

                def v_in(g, buf):
                    if not at_start(g - 1) and not at_start(g):
                        pool.wait_ge(s["values"], (g - 1) * self.ns)
                    src = v_all[:, bass.ts(g, NQT * HG * DH)].rearrange("p (k j d) -> p k j d", k=NQT, j=HG)
                    pool.tensor_copy(v_ones[buf][:, :, :, 0:DH], src).then_inc(s["v_in"], 1)

                def store(i, qh):
                    pool.wait_ge(s["sums"], HALVES * i + qh + 1)
                    d = dram[f"o{self.a}"][bass.ds(i, 1), :, qh * G:(qh + 1) * G].rearrange("o p s -> (o p) s")
                    pool.dma_start(d, o_sums[:, qh, :]).then_inc(self.out[qh], 16)

                def iteration(i, k, more):
                    if more:
                        v_in(i + 1, (k + 1) % QB)
                    for qh in range(HALVES):
                        store(i, qh)

                for i in range(QB):
                    pool.memset(k_rows[i], 1.0)
                    for par in range(2):
                        pool.memset(q_rows[i][par], 0.0)
                    last = pool.memset(v_ones[i][:, :, :, :], 1.0)
                last.then_inc(s["ready"], 1)
                pool.wait_ge(s["ready"], 1)
                v_in(0, 0)
                iteration(0, 0, True)
                with pool.Fori(0, (NG - 2) // QB) as r:
                    for k in range(QB):
                        iteration(QB * r + (k + 1), k + 1, True)
                for i in range((NG - 2) // QB * QB + 1, NG):
                    iteration(i, i, i + 1 < NG)
                for qh in range(HALVES):
                    pool.wait_ge(self.out[qh], 16 * NG)

        at = {a: Attention(a) for a in (1, 2)}

        first = {x: sem(f"first_{x}") for x in ("x_in", "ln_out")}
        f_outer, f_inner = Norm("first_outer", 0), Norm("first_inner", 1)
        mid = {x: sem(f"mid_{x}") for x in ("in", "x2", "T", "yT", "up", "gelu", "down", "f", "x", "out")}
        m_inner, m_outer = Norm("mid_inner", 0), Norm("mid_outer", 1)
        end = {x: sem(f"end_{x}") for x in ("in", "link", "x1", "T", "yT", "logits", "gap", "e2", "comb",
                                            "up", "gelu", "down", "sum", "y", "out")}
        e_first, e_last = Norm("end_first", 0), Norm("end_last", 1)

        def groups(eng):
            for half in range(HALVES):
                yield 0, half, half
            with eng.Fori(1, B) as b:
                for half in range(HALVES):
                    yield b, half, b * HALVES + half

        def transposes(pe, to, src):
            for g in range(GT):
                last = pe.transpose(to[:, g * P:(g + 1) * P], src[:, g, :], ident[:, :])
            return last

        class Heads:

            def __init__(self, a, name):
                self.a = a
                self.s = {x: sem(f"{name}_{x}") for x in ("tokens", "rcp", "normal", "T", "kept", "product")}

            def pe(self, pe, n):
                s = self.s
                for g in range(GT):
                    for hg in range(HG):
                        last = pe.transpose(bank[g][:, hg * P:(hg + 1) * P], heads_in[:, hg, g * P:(g + 1) * P], ident[:, :])
                last.then_inc(s["tokens"], 1)
                pe.wait_ge(s["normal"], n + 1)
                pe.wait_ge(s["kept"], n)
                transposes(pe, bank[7], heads_tok).then_inc(s["T"], 1)
                pe.wait_ge(s["kept"], n + 1)
                for g in range(GT):
                    o = bank[6][:, g * P:(g + 1) * P]
                    last = pe.matmul(o, headsT[:, g * P:(g + 1) * P], w_o[self.a][:, :], start=True, stop=(self.a == 1))
                    if self.a == 2:
                        last = pe.matmul(o, ones_row[:, :], rows[:, 1, :], start=False, stop=True)
                last.then_inc(s["product"], 1)

            def dve(self, dve, n):
                s = self.s
                dve.wait_ge(s["tokens"], n + 1)
                view = banks03[:, :, :].rearrange("p t (h c) -> p t h c", h=H)
                dve.wait_ge(s["normal"], n)
                dve.reciprocal(sums_rcp[:, :, :], view[:, :, :, DH]).then_inc(s["rcp"], 1)
                dve.wait_ge(s["rcp"], n + 1)
                dve.wait_ge(s["T"], n)
                for g in range(GT):
                    last = dve.tensor_tensor(heads_tok[:, g, :].rearrange("p (h d) -> p h d", h=H), view[:, g, :, 0:DH],
                                             sums_rcp[:, g, :].rearrange("p (h o) -> p h o", o=1).broadcast_to([P, H, DH]),
                                             ALU.mult)
                last.then_inc(s["normal"], 1)
                dve.wait_ge(s["T"], n + 1)
                dve.wait_ge(s["product"], n)
                dve.tensor_copy(headsT[:, :], bank[7]).then_inc(s["kept"], 1)

        def down_product(pe, to, h, w, bias):
            for g in range(GT):
                for f in range(FC):
                    pe.matmul(to[:, g * P:(g + 1) * P], hidden[:, h, f, g * P:(g + 1) * P], w[:, f, :],
                              start=(f == 0), stop=False)
                last = pe.matmul(to[:, g * P:(g + 1) * P], ones_row[:, :], bias, start=False, stop=True)
            return last

        m_heads, e_heads = Heads(1, "mid_heads"), Heads(2, "end_heads")

        def flat(tile):
            return tile.rearrange("p t d -> p (t d)")

        block = ctx.enter_context(nc.Block())

        loads = []

        def constant(to, src):
            loads.append((to, src))

        constant(ident[:, :], t["ident"])
        constant(ident_b[:, :], t["ident_b"])
        constant(later_keys[:, :], t["later_keys"])
        constant(later_keys_T[:, :], t["later_keys_T"])
        constant(iota_e[:, :], t["iota_e"])
        for a in (1, 2):
            constant(rope[a][:, :, :], t[f"rope{a}"])
            constant(w_qk[a][:, :, :], t[f"w_qk{a}"])
            constant(w_v[a][:, :], t[f"w_v{a}"])
            constant(w_o[a][:, :], t[f"w_o{a}"])
        constant(b_qk[:, :], t["b_qk"])
        for i, x in enumerate(("bv", "bo", "b2")):
            constant(rows[:, i, :], t[x].rearrange("(o d) -> o d", o=1))
        constant(rows[:, 4:4 + E, :], t["eb2"].rearrange("(o e) d -> o e d", o=1))
        constant(bg_row[:, :], t["bg"].rearrange("(o e) -> o e", o=1))
        for i, x in enumerate(("ln1_g", "ln1_b", "ln2_g", "ln2_b")):
            constant(cols1[:, i:i + 1], t[x].rearrange("(d o) -> d o", o=1))
        for i, x in enumerate(("g1", "be1", "g2", "be2")):
            constant(ln_rows[:, i, :], t[x].rearrange("(o d) -> o d", o=1).broadcast_to([P, D]))
        constant(w1[:, :], t["w1"])
        constant(b1c[:, :], t["b1c"])
        constant(w2[:, :, :], t["w2"].rearrange("(f p) d -> p f d", p=P))
        constant(wg[:, :], t["wg"])
        constant(ew1[:, :, :], t["ew1"].rearrange("e d f -> d e f"))
        constant(eb1[:, :, :], t["eb1c"])
        constant(ew2[:, :, :, :], t["ew2"].rearrange("e (f p) d -> p e f d", p=P))

        def ready(eng):
            eng.wait_ge(loaded, 16 * len(loads))
            eng.wait_ge(set_up, 1)

        @block.sync
        def _(sp):
            for to, src in loads:
                sp.dma_start(to, src).then_inc(loaded, 16)
            for b, half, n in groups(sp):
                sp.wait_ge(f_outer.done, 5 * n + 5)
                sp.dma_start(tokens(x_ln_d, b, half), xb).then_inc(first["ln_out"], 16)
                proj[1].sp(sp, n, b, half)
            sp.wait_ge(first["ln_out"], 16 * B * HALVES)
            sp.wait_ge(proj[1].s["stored"], N_STORES * B * HALVES)
            barrier(sp, 1)
            at[1].sp(sp)
            barrier(sp, 2)
            for b, half, n in groups(sp):
                sp.wait_ge(mid["x"], n + 1)
                sp.dma_start(tokens(x_mid_d, b, half), xf).then_inc(mid["out"], 16)
                sp.wait_ge(m_outer.done, 5 * n + 5)
                sp.dma_start(tokens(z_d, b, half), xz).then_inc(mid["out"], 16)
                proj[2].sp(sp, n, b, half)
            sp.wait_ge(mid["out"], 32 * B * HALVES)
            sp.wait_ge(proj[2].s["stored"], N_STORES * B * HALVES)
            barrier(sp, 3)
            at[2].sp(sp)
            barrier(sp, 4)
            for b, half, n in groups(sp):
                sp.wait_ge(end["y"], n + 1)
                sp.dma_start(tokens(x_out, b, half), xa).then_inc(end["out"], 16)
            sp.wait_ge(end["out"], 16 * B * HALVES)

        @block.gpsimd
        def _(pool):
            pool.memset(ones_row[:, :], 1.0)
            pool.memset(eps_col[:, :], EPS)
            pool.memset(e_base[:, :], float(np.exp(1.0)))
            pool.memset(minus_half[:, :], -0.5).then_inc(set_up, 1)
            ready(pool)
            for b, half, n in groups(pool):
                pool.wait_ge(f_outer.done, 5 * n)
                pool.dma_start(xt, tokens(x_in, b, half)).then_inc(first["x_in"], 16)
                f_outer.root(pool, n)
                f_inner.root(pool, n)
            barrier(pool, 1)
            at[1].pool(pool)
            barrier(pool, 2)
            for b, half, n in groups(pool):
                pool.wait_ge(mid["x"], n)
                pool.dma_start(heads_in[:, :, :], dram["o1"][bass.ds(b * HG, HG), :, half * G:(half + 1) * G]
                               .rearrange("g p s -> p g s")).then_inc(mid["in"], 16)
                pool.dma_start(xb, tokens(x_ln_d, b, half)).then_inc(mid["in"], 16)
                pool.dma_start(xt, tokens(x_in, b, half)).then_inc(mid["in"], 16)
                m_inner.root(pool, n)
                m_outer.root(pool, n)
            barrier(pool, 3)
            at[2].pool(pool)
            barrier(pool, 4)
            for b, half, n in groups(pool):
                pool.wait_ge(end["y"], n)
                pool.dma_start(heads_in[:, :, :], dram["o2"][bass.ds(b * HG, HG), :, half * G:(half + 1) * G]
                               .rearrange("g p s -> p g s")).then_inc(end["in"], 16)
                pool.dma_start(xb, tokens(z_d, b, half)).then_inc(end["in"], 16)
                pool.dma_start(xt, tokens(x_mid_d, b, half)).then_inc(end["in"], 16)
                e_first.root(pool, n)
                pool.wait_ge(end["gap"], n + 1)
                pool.tensor_tensor(e2[:, :], e_base[:, :], gap[:, :], ALU.pow).then_inc(end["e2"], 1)
                e_last.root(pool, n)

        @block.tensor
        def _(pe):
            ready(pe)
            for b, half, n in groups(pe):
                proj[1].pe(pe, n, xz, f_inner.done, 5 * n + 5)
            barrier(pe, 1)
            at[1].pe(pe)
            barrier(pe, 2)
            for b, half, n in groups(pe):
                pe.wait_ge(mid["in"], 48 * (n + 1))
                pe.wait_ge(mid["f"], n)
                pe.wait_ge(proj[2].s["products"], n)
                pe.wait_ge(mid["yT"], n)
                m_heads.pe(pe, n)
                pe.wait_ge(m_inner.done, 5 * n + 5)
                transposes(pe, bank[7], xd).then_inc(mid["T"], 1)
                pe.wait_ge(mid["yT"], n + 1)
                for f in range(FC):
                    pe.matmul(bank[f], w1[:, f * P:(f + 1) * P], yT[:, :], start=True, stop=True).then_inc(mid["up"], 1)
                pe.wait_ge(mid["gelu"], FC * (n + 1))
                down_product(pe, bank[6], 0, w2, rows[:, 2, :]).then_inc(mid["down"], 1)
                proj[2].pe(pe, n, xz, m_outer.done, 5 * n + 5)
            barrier(pe, 3)
            at[2].pe(pe)
            barrier(pe, 4)
            for b, half, n in groups(pe):
                pe.wait_ge(end["in"], 48 * (n + 1))
                pe.wait_ge(end["sum"], E * n)
                pe.wait_ge(end["gelu"], FC * E * n)
                pe.wait_ge(end["yT"], n)
                e_heads.pe(pe, n)
                pe.wait_ge(end["x1"], n + 1)
                transposes(pe, bank[7], xf).then_inc(end["T"], 1)
                pe.wait_ge(end["yT"], n + 1)
                for g in range(GT):
                    o = bank[5][:, g * E:(g + 1) * E]
                    pe.matmul(o, yT[:, g * P:(g + 1) * P], wg[:, :], start=True, stop=False)
                    last = pe.matmul(o, ones_row[:, :], bg_row[:, :], start=False, stop=True)
                last.then_inc(end["logits"], 1)

                def up(e):
                    for f in range(FC):
                        if e:
                            pe.wait_ge(end["gelu"], FC * (E * n + e - 1) + f + 1)
                        pe.matmul(bank[f], ew1[:, e, f * P:(f + 1) * P], yT[:, :], start=True,
                                  stop=True).then_inc(end["up"], 1)

                up(0)
                for e in range(E):
                    if e + 1 < E:
                        up(e + 1)
                    pe.wait_ge(end["gelu"], FC * (E * n + e + 1))
                    if e >= 2:
                        pe.wait_ge(end["sum"], E * n + e - 1)
                    down_product(pe, bank[4 + 2 * (e % 2)], e % 2, ew2[:, e, :, :],
                                 rows[:, 4 + e, :]).then_inc(end["down"], 1)

        @block.vector
        def _(dve):
            ready(dve)
            for b, half, n in groups(dve):
                dve.wait_ge(first["x_in"], 16 * (n + 1))
                f_outer.statistics(dve, n, xt)
                dve.wait_ge(first["ln_out"], 16 * n)
                f_outer.apply(dve, n, xb, xt)
                dve.wait_ge(f_outer.done, 5 * n + 5)
                f_inner.statistics(dve, n, xb)
                dve.wait_ge(proj[1].s["zT"], n)
                f_inner.apply(dve, n, xz, xb)
                proj[1].dve(dve, n, half)
            barrier(dve, 1)
            at[1].dve(dve)
            barrier(dve, 2)
            for b, half, n in groups(dve):
                dve.wait_ge(mid["in"], 48 * (n + 1))
                m_heads.dve(dve, n)
                dve.wait_ge(m_heads.s["product"], n + 1)
                dve.tensor_tensor(flat(xc), bank[6], flat(xb), ALU.add).then_inc(mid["x2"], 1)
                dve.wait_ge(mid["x2"], n + 1)
                m_inner.statistics(dve, n, xc)
                m_inner.apply(dve, n, xd, xc)
                dve.wait_ge(mid["T"], n + 1)
                dve.tensor_scalar(yT[:, :], bank[7], cols1[:, 2:3], cols1[:, 3:4], ALU.mult, ALU.add).then_inc(mid["yT"], 1)
                dve.wait_ge(mid["down"], n + 1)
                dve.tensor_tensor(flat(xe), bank[6], flat(xc), ALU.add).then_inc(mid["f"], 1)
                dve.wait_ge(mid["f"], n + 1)
                dve.wait_ge(mid["out"], 32 * n)
                dve.tensor_tensor(flat(xf), flat(xe), flat(xt), ALU.add).then_inc(mid["x"], 1)
                dve.wait_ge(mid["x"], n + 1)
                m_outer.statistics(dve, n, xf)
                dve.wait_ge(proj[2].s["zT"], n)
                m_outer.apply(dve, n, xz, xf)
                proj[2].dve(dve, n, half)
            barrier(dve, 3)
            at[2].dve(dve)
            barrier(dve, 4)
            LINKS = 13
            for b, half, n in groups(dve):
                links = [0]

                def link(ins):
                    links[0] += 1
                    ins.then_inc(end["link"], 1)
                    dve.wait_ge(end["link"], LINKS * n + links[0])

                def rows_of(i):
                    return ln_rows[:, i:i + 1, :].broadcast_to([P, GT, D])

                dve.wait_ge(end["in"], 48 * (n + 1))
                e_heads.dve(dve, n)
                dve.wait_ge(e_heads.s["product"], n + 1)
                link(dve.tensor_tensor(flat(xc), bank[6], flat(xb), ALU.add))
                e_first.statistics(dve, n, xc)
                e_first.apply(dve, n, xd, xc)
                dve.wait_ge(e_first.done, 5 * n + 5)
                link(dve.tensor_tensor(xe, xd, rows_of(0), ALU.mult))
                dve.wait_ge(end["T"], n)
                dve.tensor_tensor(xf, xe, rows_of(1), ALU.add).then_inc(end["x1"], 1)
                dve.wait_ge(end["T"], n + 1)
                dve.wait_ge(end["up"], E * FC * n)
                dve.tensor_copy(yT[:, :], bank[7]).then_inc(end["yT"], 1)
                dve.wait_ge(end["logits"], n + 1)
                link(dve.tensor_copy(gate[:, :, :].rearrange("p t e -> p (t e)"), bank[5][:, 0:GT * E]))
                carry_wait(dve)
                for g in range(GT):
                    last = dve.max(top[:, g, :], gate[:, g, :])
                link(last)
                carry_wait(dve)
                for g in range(GT):
                    last = dve.max_index(top_i[:, g, :], top[:, g, :], gate[:, g, :])
                link(last)
                dve.tensor_tensor(gap[:, :], top[:, :, 1], top[:, :, 0], ALU.subtract).then_inc(end["gap"], 1)
                link(dve.tensor_copy(top_f[:, :, :], top_i[:, :, 0:2]))
                dve.wait_ge(end["e2"], n + 1)
                link(dve.tensor_scalar(esum[:, :], e2[:, :], 1.0, 0.0, ALU.add, ALU.add))
                link(dve.reciprocal(pw[:, :, 0], esum[:, :]))
                link(dve.tensor_tensor(pw[:, :, 1], e2[:, :], pw[:, :, 0], ALU.mult))
                for g in range(GT):
                    for i in range(2):
                        last = dve.tensor_scalar(comb[:, i, g, :], iota_e[:, :], top_f[:, g, i:i + 1], pw[:, g, i:i + 1],
                                                 ALU.is_equal, ALU.mult)
                link(last)
                link(dve.tensor_tensor(comb[:, 0, :, :], comb[:, 0, :, :], comb[:, 1, :, :], ALU.add))
                dve.wait_ge(end["out"], 16 * n)
                for e in range(E):
                    dve.wait_ge(end["down"], E * n + e + 1)
                    if e:
                        dve.wait_ge(end["sum"], E * n + e)
                    for g in range(GT):
                        last = dve.scalar_tensor_tensor(xa[:, g, :], bank[4 + 2 * (e % 2)][:, g * P:(g + 1) * P],
                                                        comb[:, 0, g, e:e + 1], (xa if e else xf)[:, g, :], ALU.mult, ALU.add)
                    last.then_inc(end["sum"], 1)
                dve.wait_ge(end["sum"], E * (n + 1))
                e_last.statistics(dve, n, xa)
                e_last.apply(dve, n, xz, xa)
                dve.wait_ge(e_last.done, 5 * n + 5)
                link(dve.tensor_tensor(xc, xz, rows_of(2), ALU.mult))
                link(dve.tensor_tensor(xe, xc, rows_of(3), ALU.add))
                assert links[0] == LINKS
                dve.tensor_tensor(flat(xa), flat(xe), flat(xt), ALU.add).then_inc(end["y"], 1)

        @block.scalar
        def _(act):
            ready(act)
            for b, half, n in groups(act):
                proj[1].act(act, n, b, half)
            barrier(act, 1)
            at[1].act(act)
            barrier(act, 2)
            for b, half, n in groups(act):
                for f in range(FC):
                    act.wait_ge(mid["up"], FC * n + f + 1)
                    act.wait_ge(mid["down"], n)
                    act.activation(hidden[:, 0, f, :], bank[f], ACT.Gelu, bias=b1c[:, f:f + 1]).then_inc(mid["gelu"], 1)
                proj[2].act(act, n, b, half)
            barrier(act, 3)
            at[2].act(act)
            barrier(act, 4)
            for b, half, n in groups(act):
                for e in range(E):
                    for f in range(FC):
                        act.wait_ge(end["up"], FC * (E * n + e) + f + 1)
                        if e >= 2:
                            act.wait_ge(end["down"], E * n + e - 1)
                        else:
                            act.wait_ge(end["down"], E * n)
                        act.activation(hidden[:, e % 2, f, :], bank[f], ACT.Gelu,
                                       bias=eb1[:, e, f:f + 1]).then_inc(end["gelu"], 1)


def _rope_tables(half_split):
    inv = (np.float32(10000.0) ** (-(np.arange(0, DH, 2, dtype=np.float32) / np.float32(DH)))).astype(np.float32)
    theta = np.arange(S, dtype=np.float32)[:, None] * inv[None, :]
    table = np.zeros((P, 2, S), np.float32)
    for r in range(P):
        d = r % 32 % 16 // 2
        angle, negative = (d % (DH // 2), d < DH // 2) if half_split else (d // 2, d % 2 == 0)
        table[r, 0] = np.cos(theta[:, angle])
        table[r, 1] = np.sin(theta[:, angle]) * np.float32(-1 if negative else 1)
    return table


def _columns(half_split):
    own, partner = [], []
    for r in range(P):
        hg, par, d, pair = r // 32, r % 32 // 16, r % 16 // 2, r % 2
        head = hg * HG + pair * 2 + par
        own.append(head * DH + d)
        partner.append(head * DH + ((d + DH // 2) % DH if half_split else d ^ 1))
    return own, partner


def kernel(**inputs):
    import concourse.bacc as bacc
    from concourse.bass_utils import run_bass_kernel_spmd

    a = {k.replace("L0_", ""): np.asarray(v) for k, v in inputs.items()}
    bf = mybir.dt.np(BF16)
    heads = np.arange(P)
    later = np.where(heads[None, :] > heads[:, None], LOW, 0.0)
    arrays = {
        "x": a["attn_x"],
        "ident": np.eye(P, dtype=np.float32), "ident_b": np.eye(P).astype(bf),
        "later_keys": later.astype(bf), "later_keys_T": later.T.astype(bf),
        "iota_e": np.tile(np.arange(E, dtype=np.float32), (P, 1)),
        "rope1": _rope_tables(False), "rope2": _rope_tables(True),
    }
    own, partner = _columns(False)
    q, k, v = (a["attn_Wqkv"][:, i * D:(i + 1) * D] for i in range(3))
    arrays["w_qk1"] = np.stack([q[:, own], q[:, partner], k[:, own], k[:, partner]], axis=1)
    arrays["w_v1"] = v
    own, partner = _columns(True)
    q, k = a["ffn_Wq"], a["ffn_Wk"]
    arrays["w_qk2"] = np.stack([q[:, own], q[:, partner], k[:, own], k[:, partner]], axis=1)
    q, k = a["ffn_bq"], a["ffn_bk"]
    arrays["b_qk"] = np.stack([q[own], q[partner], k[own], k[partner]], axis=1)
    arrays["w_v2"] = a["ffn_Wv"]
    arrays["w_o1"], arrays["w_o2"] = a["attn_Wo"], a["ffn_Wo"]
    for x in ("ln1_g", "ln1_b", "ln2_g", "ln2_b"):
        arrays[x] = a["attn_" + x]
    for x, y in (("bv", "bv"), ("bo", "bo"), ("bg", "bg"), ("wg", "Wg"), ("g1", "g1"), ("be1", "be1"), ("g2", "g2"),
                 ("be2", "be2"), ("ew1", "W1"), ("ew2", "W2"), ("eb2", "b2")):
        arrays[x] = a["ffn_" + y]
    arrays["w1"], arrays["w2"], arrays["b2"] = a["attn_W1"], a["attn_W2"], a["attn_b2"]
    arrays["b1c"] = a["attn_b1"].reshape(FC, P).T
    arrays["eb1c"] = a["ffn_b1"].reshape(E, FC, P).transpose(2, 0, 1)
    arrays = {f"in_{k}": np.ascontiguousarray(v) for k, v in arrays.items()}

    nc = bacc.Bacc("TRN2", target_bir_lowering=False, num_devices=1)
    t = {k[3:]: nc.dram_tensor(k, v.shape, mybir.dt.from_np(v.dtype), kind="ExternalInput").ap() for k, v in arrays.items()}
    out = nc.dram_tensor("out_x", (B, S, D), F32, kind="ExternalOutput").ap()
    build(nc, t, out)
    return run_bass_kernel_spmd(nc, [arrays], core_ids=[0]).results[0]["out_x"]
```

```python
from contextlib import ExitStack

import numpy as np

import concourse.bass as bass
from concourse import mybir

F32 = mybir.dt.float32
BF16 = mybir.dt.bfloat16
U32 = mybir.dt.uint32
ALU = mybir.AluOpType
ACT = mybir.ActivationFunctionType
AX = mybir.AxisListType

P = 128
B, S, D = 4, 1024, 128
H, DH = 16, 8
E, FF = 8, 512
FC = FF // P
HG = 4
NG = B * H // HG
NQT = S // P
G = 512
GT = G // P
HALVES = S // G
T = B * S
EPS = 1e-5
SCALE = float(DH) ** -0.5
LOW = -3.0e38
Q_SLOTS = (0, 0, 1, 1, 0, 2)
K_SLOTS = (0, 1, 0, 1, 2, 0)
NS = len(Q_SLOTS)
KS = NS * DH
M0 = 2 * KS
NRING = 8
QB = 3
LEAD = 12
COVER = 4
CHUNK_BANKS = (4, 5, 7)


def at(i, group):
    return isinstance(i, int) and i == group


def beyond(i):
    return isinstance(i, int) and i >= NG


def attention_plan(causal):
    chunks = []
    for qt in range(NQT):
        for kh in range(HALVES):
            width = min(G, (qt + 1) * P - kh * G) if causal else G
            if width <= 0:
                continue
            masked = causal and kh == qt // GT
            for pair in range(2):
                for par in range(2):
                    chunks.append((qt, pair, par, kh, width, masked))
    steps = []
    for qh in range(HALVES):
        n = (qh + 1) * GT if causal else NQT
        for kt in range(n):
            diagonal = causal and kt >= qh * GT
            steps.append((qh, kt, (kt - qh * GT) * P if diagonal else 0, diagonal, kt == 0, kt == n - 1))
    n = len(chunks)
    stream = [("chunk", 1, c) for c in range(LEAD, n)] + [("maxima", 1, 0)]
    stream += [("chunk", 2, c) for c in range(LEAD)]
    stream.insert(n - LEAD + 1 + COVER, ("transposes", 1, 0))
    order, c = [], 0

    def some(upto):
        nonlocal c
        while c < upto:
            order.append(stream[c])
            c += 1

    for k, step in enumerate(steps):
        for pair in range(2):
            order.append(("unit", 0, 2 * k + pair))
            some((2 * k + pair + 1) * len(stream) // (2 * len(steps)))
        if k:
            order.append(("values", 0, k - 1))
    order.append(("values", 0, len(steps) - 1))
    return chunks, steps, order


def build(nc, t, out):
    with ExitStack() as ctx:
        def sb(name, shape, dt=F32):
            return ctx.enter_context(nc.sbuf_tensor(name, shape, dt))

        def sem(name):
            return ctx.enter_context(nc.semaphore(name))

        dram = {}
        for n in (1, 2):
            for qk in "qk":
                dram[f"{qk}{n}"] = nc.dram_tensor(f"{qk}_slots{n}", [NS, NG, 2, DH, 2 * S], BF16, kind="Internal").ap()
            dram[f"o{n}"] = nc.dram_tensor(f"heads_out{n}", [NG, P, S], F32, kind="Internal").ap()
        x_ln_d = nc.dram_tensor("x_ln_d", [T, D], F32, kind="Internal").ap()
        x_mid_d = nc.dram_tensor("x_mid_d", [T, D], F32, kind="Internal").ap()
        z_d = nc.dram_tensor("z_d", [T, D], F32, kind="Internal").ap()
        x_in = t["x"].rearrange("b s d -> (b s) d")
        x_out = out.rearrange("b s d -> (b s) d")

        def tokens(dram_ap, b, half):
            return dram_ap[bass.ds(b * S + half * G, G), :].rearrange("(t p) d -> p t d", p=P)

        ident = sb("ident", [P, P])
        ident_b = sb("ident_b", [P, P], BF16)
        later_keys = sb("later_keys", [P, P], BF16)
        later_keys_T = sb("later_keys_T", [P, P], BF16)
        rope = {n: sb(f"rope{n}", [P, 2, S]) for n in (1, 2)}
        w_qk = {n: sb(f"w_qk{n}", [P, 4, P]) for n in (1, 2)}
        w_v = {n: sb(f"w_v{n}", [P, P]) for n in (1, 2)}
        w_o = {n: sb(f"w_o{n}", [P, P]) for n in (1, 2)}
        b_qk = sb("b_qk", [P, 4])
        rows = sb("rows", [1, 4 + E, P])
        bg_row = sb("bg_row", [1, E])
        cols1 = sb("cols1", [P, 4])
        ln_rows = sb("ln_rows", [P, 4, P])
        w1 = sb("w1", [P, FF])
        b1c = sb("b1c", [P, FC])
        w2 = sb("w2", [P, FC, P])
        wg = sb("wg", [P, E])
        ew1 = sb("ew1", [P, E, FF])
        eb1 = sb("eb1", [P, E, FC])
        ew2 = sb("ew2", [P, E, FC, P])
        ones_row = sb("ones_row", [1, P])
        minus_half = sb("minus_half", [P, GT])
        e_base = sb("e_base", [P, GT])
        eps_col = sb("eps_col", [P, GT])
        carrier = sb("carrier", [P, 1])
        iota_e = sb("iota_e", [P, E])

        heads_in = sb("heads_in", [P, HG, G])
        heads_tok = sb("heads_tok", [P, GT, D])
        sums_rcp = sb("sums_rcp", [P, GT, H])
        headsT = sb("headsT", [P, G])
        yT = sb("yT", [P, G])
        hT = sb("hT", [P, G])
        stats = sb("stats", [P, 2, GT, 6])
        mv = sb("mv", [P, 2, GT, 2])
        ve = sb("ve", [P, 2, GT])
        rstd = sb("rstd", [P, 2, GT])
        parts = sb("parts", [P, 3, 2, G], BF16)
        v_all = sb("v_all", [P, NG * NQT * HG * DH])
        gate = sb("gate", [P, GT, E])
        top = sb("top", [P, GT, 8])
        top_i = sb("top_i", [P, GT, 8], U32)
        top_f = sb("top_f", [P, GT, 2])
        gap = sb("gap", [P, GT])
        e2 = sb("e2", [P, GT])
        esum = sb("esum", [P, GT])
        pw = sb("pw", [P, GT, 2])
        comb = sb("comb", [P, 2, GT, E])
        weights = sb("weights", [P, HALVES, GT, E])

        k_work = sb("k_work", [P, QB, 2 * S], BF16)
        k_rows = [k_work[:, i, :].rearrange("p (l s) -> p l s", l=2) for i in range(QB)]
        q_work = sb("q_work", [P, QB, 2, 2 * S], BF16)
        q_rows = [[q_work[:, i, par, :].rearrange("p (l s) -> p l s", l=2) for par in range(2)] for i in range(QB)]
        x_work = k_work[:, :, :].bitcast(F32).rearrange("p i (l t d) -> p (i l) t d", l=2, t=GT)
        xt, xb, xc, xd, xe, xf = (x_work[:, i, :, :] for i in range(2 * QB))
        xz = sb("xz", [P, GT, D])[:, :, :]
        xa = sb("xa", [P, GT, D])[:, :, :]
        v_ones = [sb(f"v_ones{i}", [P, NQT, HG, 32]) for i in range(QB)]
        probs = sb("probs", [P, NRING, 2, G])
        hidden = probs[:, :, 0, :].rearrange("p (h f) s -> p h f s", h=2)
        t_cos, t_sin, rot, rest = (probs[:, 2 * i:2 * i + 2, 1, :] for i in range(4))
        row_max = sb("row_max", [P, NQT, HG, HALVES])
        top_max = sb("top_max", [P, NQT * HG])
        max_rest = sb("max_rest", [P, 2, NQT * HG])
        max_parts = sb("max_parts", [P, NQT, HG, 3], BF16)
        max_T = sb("max_T", [HG * 3, S], BF16)
        o_sums = sb("o_sums", [P, HALVES, G])

        banks03 = ctx.enter_context(nc.psum_tensor("banks03", [P, 4, G], F32))
        bank = [banks03[:, i, :] for i in range(4)]
        bank += [ctx.enter_context(nc.psum_tensor(f"bank{i}", [P, G], F32))[:, :] for i in range(4, 8)]

        loaded = sem("loaded")
        loaded_late = sem("loaded_late")
        set_up = sem("set_up")
        phase = sem("phase")

        def barrier(eng, n):
            eng.drain().then_inc(phase, 1)
            eng.wait_ge(phase, 5 * n)

        def carry_wait(dve):
            dve.memset(carrier[:, :], 0.0)

        class Norm:

            def __init__(self, name, slot):
                self.done = sem(name)
                self.slot = slot

            def statistics(self, dve, n, src):
                i = self.slot
                if n is not None:
                    dve.wait_ge(self.done, 5 * n)
                for g in range(GT):
                    last = dve.bn_stats(stats[:, i, g, :], src[:, g, :])
                last.then_inc(self.done, 1)
                dve.wait_ge(self.done, 5 * n + 1)
                carry_wait(dve)
                for g in range(GT):
                    last = dve.bn_aggr(mv[:, i, g, :], stats[:, i, g, :])
                last.then_inc(self.done, 1)

            def root(self, pool, n):
                i = self.slot
                pool.wait_ge(self.done, 5 * n + 2)
                pool.tensor_tensor(ve[:, i, :], mv[:, i, :, 1], eps_col[:, :], ALU.add).then_inc(self.done, 1)
                pool.wait_ge(self.done, 5 * n + 3)
                pool.tensor_tensor(rstd[:, i, :], ve[:, i, :], minus_half[:, :], ALU.pow).then_inc(self.done, 1)

            def apply(self, dve, n, dst, src):
                i = self.slot
                dve.wait_ge(self.done, 5 * n + 4)
                for g in range(GT):
                    last = dve.tensor_scalar(dst[:, g, :], src[:, g, :], mv[:, i, g, 0:1], rstd[:, i, g:g + 1],
                                             ALU.subtract, ALU.mult)
                last.then_inc(self.done, 1)

        class Project:

            def __init__(self, a):
                self.a = a
                names = ("zT", "hT", "qk", "v", "v_kept", "products", "rot", "high", "rest", "middle", "low", "stored")
                self.s = {x: sem(f"project{a}_{x}") for x in names}

            def pe(self, pe, n, z, z_sem, z_value):
                s, a = self.s, self.a
                pe.wait_ge(z_sem, z_value)
                pe.wait_ge(s["hT"], n)
                for g in range(GT):
                    last = pe.transpose(bank[5][:, g * P:(g + 1) * P], z[:, g, :], ident[:, :])
                last.then_inc(s["zT"], 1)
                pe.wait_ge(s["hT"], n + 1)
                pe.wait_ge(s["products"], n)
                for i in range(4):
                    pe.matmul(bank[i], w_qk[a][:, i, :], hT[:, :], start=True, stop=True).then_inc(s["qk"], 1)
                pe.wait_ge(s["v_kept"], n)
                for g in range(GT):
                    o = bank[4][:, g * P:(g + 1) * P]
                    last = pe.matmul(o, hT[:, g * P:(g + 1) * P], w_v[a][:, :], start=True, stop=(a == 1))
                    if a == 2:
                        last = pe.matmul(o, ones_row[:, :], rows[:, 0, :], start=False, stop=True)
                last.then_inc(s["v"], 1)

            def dve_tokens(self, dve, n):
                s, a = self.s, self.a
                dve.wait_ge(s["zT"], n + 1)
                dve.wait_ge(s["v"], n)
                if a == 1:
                    dve.tensor_scalar(hT[:, :], bank[5], cols1[:, 0:1], cols1[:, 1:2], ALU.mult, ALU.add).then_inc(s["hT"], 1)
                else:
                    dve.tensor_copy(hT[:, :], bank[5]).then_inc(s["hT"], 1)

            def dve_parts(self, dve, n, half):
                s, a = self.s, self.a
                dve.wait_ge(s["rot"], n)
                for i in range(4):
                    dve.wait_ge(s["qk"], 4 * n + i + 1)
                    to = (t_cos, t_sin)[i % 2][:, i // 2, :]
                    table = rope[a][:, i % 2, half * G:(half + 1) * G]
                    if a == 1:
                        last = dve.tensor_tensor(to, bank[i], table, ALU.mult)
                    else:
                        last = dve.scalar_tensor_tensor(to, bank[i], b_qk[:, i:i + 1], table, ALU.add, ALU.mult)
                last.then_inc(s["products"], 1)
                dve.wait_ge(s["products"], n + 1)
                dve.wait_ge(s["rest"], n)
                dve.tensor_tensor(rot[:, :, :], t_cos[:, :, :], t_sin[:, :, :], ALU.add).then_inc(s["rot"], 1)
                dve.wait_ge(s["high"], n + 1)
                dve.wait_ge(s["low"], n)
                dve.tensor_tensor(rest[:, :, :], rot[:, :, :], parts[:, 0, :, :], ALU.subtract).then_inc(s["rest"], 1)
                dve.wait_ge(s["middle"], n + 1)
                dve.tensor_tensor(parts[:, 2, :, :], rest[:, :, :], parts[:, 1, :, :], ALU.subtract).then_inc(s["low"], 1)

            def act(self, act, n, b, half):
                s = self.s
                act.wait_ge(s["rot"], n + 1)
                act.wait_ge(s["stored"], n * N_STORES)
                act.activation(parts[:, 0, :, :], rot[:, :, :], ACT.Copy).then_inc(s["high"], 1)
                act.wait_ge(s["v"], n + 1)
                to = v_all[:, bass.ts(b, S)].rearrange("p (h k c) -> p k h c", h=H // HG, k=NQT)
                act.activation(to[:, half * GT:(half + 1) * GT, :, :],
                               bank[4].rearrange("p (k h c) -> p k h c", k=GT, h=H // HG), ACT.Copy).then_inc(s["v_kept"], 1)
                act.wait_ge(s["rest"], n + 1)
                act.activation(parts[:, 1, :, :], rest[:, :, :], ACT.Copy).then_inc(s["middle"], 1)

            def sp(self, sp, n, b, half):
                s, a = self.s, self.a
                for part, ready in ((0, "high"), (1, "middle"), (2, "low")):
                    sp.wait_ge(s[ready], n + 1)
                    for qk, slots in enumerate((Q_SLOTS, K_SLOTS)):
                        for slot in range(NS):
                            if slots[slot] != part:
                                continue
                            d = dram["qk"[qk] + str(a)][slot, bass.ts(b, H // HG), :, :, :]
                            d = d.rearrange("g r d (l s) -> (g r d l) s", l=2)
                            sp.dma_start(d[:, half * G:(half + 1) * G], parts[:, part, qk, :]).then_inc(s["stored"], 16)

        N_STORES = 2 * NS * 16
        proj = {a: Project(a) for a in (1, 2)}

        class Attention:

            def __init__(self, a):
                self.a = a
                self.causal = a == 1
                self.chunks, self.steps, self.order = attention_plan(self.causal)
                self.slots = [event for event in self.order if event[0] in ("chunk", "transposes")]
                assert QB * len(self.slots) % len(CHUNK_BANKS) == 0 and LEAD >= len(CHUNK_BANKS)
                self.nc, self.ns, self.nu = len(self.chunks), len(self.steps), 2 * len(self.steps)
                names = ("v_in", "chunk", "chunk_max", "maxima", "max_T", "max_out", "max_in",
                         "scores", "exps", "values", "sums", "ready", "cleared")
                self.s = {x: sem(f"attend{a}_{x}") for x in names}
                self.rows_in = [sem(f"attend{a}_rows_in{i}") for i in range(QB)]
                self.out = [sem(f"attend{a}_out{i}") for i in range(HALVES)]

            def chunk_bank(self, slot, k):
                return bank[CHUNK_BANKS[(LEAD + (k + 1) * len(self.slots) + slot) % len(CHUNK_BANKS)]]

            def load(self, sp, i, buf):
                for tile, name in ((q_rows, "q"), (k_rows, "k")):
                    for par in range(2):
                        src = dram[f"{name}{self.a}"][:, bass.ds(i, 1), par, :, :].rearrange("n o d s -> n (o d) s")
                        to = tile[buf] if name == "k" else tile[buf][par]
                        sp.dma_start(to[par * KS:(par + 1) * KS, :, :].rearrange("p l s -> p (l s)"), src).then_inc(self.rows_in[buf], 16)

            def sp_maxima(self, sp, i, buf):
                sp.wait_ge(self.s["max_out"], i + 1)
                for j in range(HG):
                    pair, par = divmod(j, 2)
                    sp.dma_start(q_rows[buf][par][M0:M0 + 3, pair, :],
                                 max_T[3 * j:3 * j + 3, :]).then_inc(self.s["max_in"], 16)

            def sp(self, sp):
                for i in range(QB):
                    self.load(sp, i, i)
                self.sp_maxima(sp, 0, 0)

                def iteration(i, k, load):
                    self.sp_maxima(sp, i + 1, (k + 1) % QB)
                    if load:
                        sp.wait_ge(self.s["scores"], (i + 1) * self.nu)
                        self.load(sp, i + QB, k % QB)

                with sp.Fori(0, (NG - QB - 1) // QB) as r:
                    for k in range(QB):
                        iteration(QB * r + k, k, True)
                for i in range((NG - QB - 1) // QB * QB, NG - 1):
                    iteration(i, i, i + QB < NG)

            def pe(self, pe):
                s = self.s

                def free(g, slot):
                    before = slot - len(CHUNK_BANKS)
                    if before >= 0:
                        what, ahead, c = self.slots[before]
                        g = g + ahead - self.slots[slot][1]
                    else:
                        what, ahead, c = self.slots[before + len(self.slots)]
                        g = g + ahead - 1 - self.slots[slot][1]
                    if beyond(g):
                        return
                    if what == "chunk":
                        pe.wait_ge(s["chunk_max"], g * self.nc + c + 1)
                    else:
                        pe.wait_ge(s["max_out"], g + 1)

                def chunk(g, c, buf, turn, to):
                    qt, pair, par, kh, width, masked = self.chunks[c]
                    if c == 0:
                        pe.wait_ge(self.rows_in[buf], 64 * (turn + 1))
                    last = pe.matmul(to[:, 0:width], q_rows[buf][par][0:M0, pair, qt * P:(qt + 1) * P],
                                     k_rows[buf][0:M0, pair, kh * G:kh * G + width], start=True, stop=not masked)
                    if masked:
                        last = pe.matmul(to[:, width - P:width], ident_b[:, :], later_keys[:, :],
                                         start=False, stop=True)
                    last.then_inc(s["chunk"], 1)

                def maxima(g, to):
                    pe.wait_ge(s["maxima"], 5 * (g + 1))
                    view = to.bitcast(BF16)
                    for qt in range(NQT):
                        last = pe.transpose(view[0:3 * HG, qt * P:(qt + 1) * P],
                                            max_parts[:, qt, :, :].rearrange("p j c -> p (j c)"), ident_b[:, :])
                    last.then_inc(s["max_T"], 1)

                def unit(i, u, buf):
                    qh, kt, c0, masked, *_ = self.steps[u // 2]
                    pair = u % 2
                    if u == 0:
                        pe.wait_ge(s["max_in"], 64 * (i + 1))
                    if u >= 2 or not at(i, 0):
                        pe.wait_ge(s["exps"], i * self.nu + u - 1)
                    for par in range(2):
                        last = pe.matmul(bank[2 * (u % 2) + par][:, 0:G - c0], k_rows[buf][:, pair, kt * P:(kt + 1) * P],
                                         q_rows[buf][par][:, pair, qh * G + c0:(qh + 1) * G], start=True, stop=not masked)
                    if masked:
                        for par in range(2):
                            last = pe.matmul(bank[2 * (u % 2) + par][:, 0:P], ident_b[:, :], later_keys_T[:, :],
                                             start=False, stop=True)
                    last.then_inc(s["scores"], 1)

                def values(i, k, buf):
                    qh, kt, c0, _, first, last_kt = self.steps[k]
                    pe.wait_ge(s["exps"], i * self.nu + 2 * k + 2)
                    if k == 0:
                        pe.wait_ge(s["v_in"], i + 1)
                    if first and (qh or not at(i, 0)):
                        pe.wait_ge(s["sums"], HALVES * i + qh)
                    for j in range(HG):
                        pair, par = divmod(j, 2)
                        last = pe.matmul(bank[6][32 * j:32 * j + 32, c0:G], v_ones[buf][:, kt, j, :],
                                         probs[:, (2 * k + pair) % NRING, par, 0:G - c0], start=first, stop=last_kt)
                    last.then_inc(s["values"], 1)

                def iteration(i, k, r=0):
                    slot = 0
                    for what, ahead, n in self.order:
                        if what == "unit" and not at(i, -1):
                            unit(i, n, k % QB)
                        if what == "values" and not at(i, -1):
                            values(i, n, k % QB)
                        if what not in ("chunk", "transposes"):
                            continue
                        if not beyond(i + ahead):
                            free(i + ahead, slot)
                            if what == "chunk":
                                chunk(i + ahead, n, (k + ahead) % QB, r + (k + ahead) // QB, self.chunk_bank(slot, k))
                            else:
                                maxima(i + ahead, self.chunk_bank(slot, k))
                        slot += 1

                pe.wait_ge(s["ready"], 1)
                for c in range(LEAD):
                    if c >= len(CHUNK_BANKS):
                        pe.wait_ge(s["chunk_max"], c + 1 - len(CHUNK_BANKS))
                    chunk(0, c, 0, 0, bank[CHUNK_BANKS[c % len(CHUNK_BANKS)]])
                iteration(-1, -1)
                iteration(0, 0)
                with pe.Fori(0, (NG - 2) // QB) as r:
                    for k in range(QB):
                        iteration(QB * r + (k + 1), k + 1, r)
                for i in range((NG - 2) // QB * QB + 1, NG):
                    iteration(i, i)

            def dve(self, dve):
                s = self.s

                def chunk(g, c, to_bank):
                    qt, pair, par, kh, width, _ = self.chunks[c]
                    n = g * self.nc + c
                    if c == 0 and not at(g, 0):
                        dve.wait_ge(s["maxima"], 5 * g)
                    dve.wait_ge(s["chunk"], n + 1)
                    to = row_max[:, qt, 2 * pair + par, kh:kh + 1]
                    src = to_bank[:, 0:width]
                    dve.tensor_reduce(to, src, AX.X, ALU.max).then_inc(s["chunk_max"], 1)

                def maxima(g):
                    dve.wait_ge(s["chunk_max"], (g + 1) * self.nc)
                    dve.tensor_reduce(top_max[:, :], row_max[:, :, :, :].rearrange("p t j h -> p (t j) h"), AX.X,
                                      ALU.max).then_inc(s["maxima"], 1)
                    dve.wait_ge(s["maxima"], 5 * g + 1)
                    if not at(g, 0):
                        dve.wait_ge(s["max_T"], g)
                    part = [max_parts[:, :, :, i] for i in range(3)]
                    tm = top_max[:, :].rearrange("p (t j) -> p t j", j=HG)
                    r0 = max_rest[:, 0, :].rearrange("p (t j) -> p t j", j=HG)
                    dve.tensor_scalar(part[0], tm, -1.0, None, ALU.mult).then_inc(s["maxima"], 1)
                    dve.wait_ge(s["maxima"], 5 * g + 2)
                    dve.scalar_tensor_tensor(r0, tm, -1.0, part[0], ALU.mult, ALU.subtract).then_inc(s["maxima"], 1)
                    dve.wait_ge(s["maxima"], 5 * g + 3)
                    dve.tensor_copy(part[1], r0).then_inc(s["maxima"], 1)
                    dve.wait_ge(s["maxima"], 5 * g + 4)
                    dve.tensor_tensor(part[2], r0, part[1], ALU.subtract).then_inc(s["maxima"], 1)

                def iteration(i, k):
                    slot = 0
                    for what, ahead, n in self.order:
                        if what == "maxima" and not beyond(i + ahead):
                            maxima(i + ahead)
                        if what not in ("chunk", "transposes"):
                            continue
                        if what == "chunk" and not beyond(i + ahead):
                            chunk(i + ahead, n, self.chunk_bank(slot, k))
                        slot += 1

                dve.memset(row_max[:, :, :, :], LOW).then_inc(s["cleared"], 1)
                dve.wait_ge(s["cleared"], 1)
                for c in range(LEAD):
                    chunk(0, c, bank[CHUNK_BANKS[c % len(CHUNK_BANKS)]])
                iteration(-1, -1)
                iteration(0, 0)
                with dve.Fori(0, (NG - 2) // QB) as r:
                    for k in range(QB):
                        iteration(QB * r + (k + 1), k + 1)
                for i in range((NG - 2) // QB * QB + 1, NG - 1):
                    iteration(i, i)

            def act(self, act):
                s = self.s

                def maxima(g, src):
                    act.wait_ge(s["max_T"], g + 1)
                    if not at(g, 0):
                        act.wait_ge(s["max_in"], 64 * g)
                    act.activation(max_T[:, :], src.bitcast(BF16)[0:3 * HG, :], ACT.Copy).then_inc(s["max_out"], 1)

                def unit(i, u):
                    _, _, c0, *_ = self.steps[u // 2]
                    act.wait_ge(s["scores"], i * self.nu + u + 1)
                    if u >= NRING or not at(i, 0):
                        act.wait_ge(s["values"], i * self.ns + (u - NRING) // 2 + 1)
                    act.activation(probs[:, u % NRING, :, 0:G - c0], banks03[:, 2 * (u % 2):2 * (u % 2) + 2, 0:G - c0],
                                   ACT.Exp, scale=SCALE).then_inc(s["exps"], 1)

                def values(i, k):
                    qh, *_, last_kt = self.steps[k]
                    if not last_kt:
                        return
                    act.wait_ge(s["values"], i * self.ns + k + 1)
                    if not at(i, 0):
                        act.wait_ge(self.out[qh], 16 * i)
                    act.activation(o_sums[:, qh, :], bank[6], ACT.Copy).then_inc(s["sums"], 1)

                turned = self.slots.index(("transposes", 1, 0))

                def iteration(i, k):
                    for what, ahead, n in self.order:
                        if what == "unit" and not at(i, -1):
                            unit(i, n)
                        if what == "values" and not at(i, -1):
                            values(i, n)
                        if what == "transposes" and not beyond(i + ahead):
                            maxima(i + ahead, self.chunk_bank(turned, k))

                iteration(-1, -1)
                iteration(0, 0)
                with act.Fori(0, (NG - 2) // QB) as r:
                    for k in range(QB):
                        iteration(QB * r + (k + 1), k + 1)
                for i in range((NG - 2) // QB * QB + 1, NG):
                    iteration(i, i)

            def pool(self, pool):
                s = self.s

                def v_in(g, buf):
                    if not at(g - 1, 0) and not at(g, 0):
                        pool.wait_ge(s["values"], (g - 1) * self.ns)
                    src = v_all[:, bass.ts(g, NQT * HG * DH)].rearrange("p (k j d) -> p k j d", k=NQT, j=HG)
                    pool.tensor_copy(v_ones[buf][:, :, :, 0:DH], src).then_inc(s["v_in"], 1)

                def store(i, qh):
                    pool.wait_ge(s["sums"], HALVES * i + qh + 1)
                    d = dram[f"o{self.a}"][bass.ds(i, 1), :, qh * G:(qh + 1) * G].rearrange("o p s -> (o p) s")
                    pool.dma_start(d, o_sums[:, qh, :]).then_inc(self.out[qh], 16)

                def iteration(i, k, more):
                    if more:
                        v_in(i + 1, (k + 1) % QB)
                    for qh in range(HALVES):
                        store(i, qh)

                pool.memset(k_work[M0:P, :, :], 1.0).then_inc(s["ready"], 1)
                pool.wait_ge(s["ready"], 1)
                v_in(0, 0)
                iteration(0, 0, True)
                with pool.Fori(0, (NG - 2) // QB) as r:
                    for k in range(QB):
                        iteration(QB * r + (k + 1), k + 1, True)
                for i in range((NG - 2) // QB * QB + 1, NG):
                    iteration(i, i, i + 1 < NG)
                for qh in range(HALVES):
                    pool.wait_ge(self.out[qh], 16 * NG)

        attend = {a: Attention(a) for a in (1, 2)}

        first = {x: sem(f"first_{x}") for x in ("x_in", "ln_out")}
        f_outer, f_inner = Norm("first_outer", 0), Norm("first_inner", 1)
        mid = {x: sem(f"mid_{x}") for x in ("in", "x2", "T", "yT", "up", "gelu", "down", "f", "x", "out")}
        m_inner, m_outer = Norm("mid_inner", 0), Norm("mid_outer", 1)
        end = {x: sem(f"end_{x}") for x in ("in", "tokens", "rcp", "normal", "T", "kept", "product", "front_link", "x1",
                                            "x1_T", "yT", "logits", "gate", "gap", "e2", "up", "gelu", "down", "sum",
                                            "tail_link", "y")}
        end_out = [sem(f"end_out{i}") for i in range(HALVES)]
        e_first, e_last = Norm("end_first", 0), Norm("end_last", 1)

        def groups(eng):
            for half in range(HALVES):
                yield 0, half, half
            with eng.Fori(1, B) as b:
                for half in range(HALVES):
                    yield b, half, b * HALVES + half

        def turns(eng):
            def batch(b, more):
                for half in range(HALVES):
                    n = b * HALVES + half
                    following = (b, half + 1, n + 1) if half + 1 < HALVES else (b + 1, 0, n + 1)
                    yield (b, half, n), following if more or half + 1 < HALVES else None

            yield from batch(0, True)
            with eng.Fori(1, B - 1) as b:
                yield from batch(b, True)
            yield from batch(B - 1, False)

        def transposes(pe, to, src):
            for g in range(GT):
                last = pe.transpose(to[:, g * P:(g + 1) * P], src[:, g, :], ident[:, :])
            return last

        class Heads:

            def __init__(self, a, name):
                self.a = a
                self.s = {x: sem(f"{name}_{x}") for x in ("tokens", "rcp", "normal", "T", "kept", "product")}

            def pe(self, pe, n):
                s = self.s
                for g in range(GT):
                    for hg in range(HG):
                        last = pe.transpose(bank[g][:, hg * P:(hg + 1) * P], heads_in[:, hg, g * P:(g + 1) * P], ident[:, :])
                last.then_inc(s["tokens"], 1)
                pe.wait_ge(s["normal"], n + 1)
                pe.wait_ge(s["kept"], n)
                transposes(pe, bank[7], heads_tok).then_inc(s["T"], 1)
                pe.wait_ge(s["kept"], n + 1)
                for g in range(GT):
                    o = bank[6][:, g * P:(g + 1) * P]
                    last = pe.matmul(o, headsT[:, g * P:(g + 1) * P], w_o[self.a][:, :], start=True, stop=(self.a == 1))
                    if self.a == 2:
                        last = pe.matmul(o, ones_row[:, :], rows[:, 1, :], start=False, stop=True)
                last.then_inc(s["product"], 1)

            def dve(self, dve, n):
                s = self.s
                dve.wait_ge(s["tokens"], n + 1)
                view = banks03[:, :, :].rearrange("p t (h c) -> p t h c", h=H)
                dve.wait_ge(s["normal"], n)
                dve.reciprocal(sums_rcp[:, :, :], view[:, :, :, DH]).then_inc(s["rcp"], 1)
                dve.wait_ge(s["rcp"], n + 1)
                dve.wait_ge(s["T"], n)
                for g in range(GT):
                    last = dve.tensor_tensor(heads_tok[:, g, :].rearrange("p (h d) -> p h d", h=H), view[:, g, :, 0:DH],
                                             sums_rcp[:, g, :].rearrange("p (h o) -> p h o", o=1).broadcast_to([P, H, DH]),
                                             ALU.mult)
                last.then_inc(s["normal"], 1)
                dve.wait_ge(s["T"], n + 1)
                dve.wait_ge(s["product"], n)
                dve.tensor_copy(headsT[:, :], bank[7]).then_inc(s["kept"], 1)

        def down_product(pe, to, h, w, bias):
            for g in range(GT):
                for f in range(FC):
                    pe.matmul(to[:, g * P:(g + 1) * P], hidden[:, h, f, g * P:(g + 1) * P], w[:, f, :],
                              start=(f == 0), stop=False)
                last = pe.matmul(to[:, g * P:(g + 1) * P], ones_row[:, :], bias, start=False, stop=True)
            return last

        m_heads = Heads(1, "mid_heads")
        x_ins = (xt, probs[:, NRING - 1, 0, :].rearrange("p (t d) -> p t d", t=GT))
        spare = [probs[:, i, 1, :].rearrange("p (t d) -> p t d", t=GT) for i in range(NRING)]
        x_mids, x_ones, sums_of = (xt, spare[0]), (xf, spare[1]), (xa, spare[2])
        tail_a, tail_b = spare[3], spare[4]
        yTs = (yT, hT)
        front_bank = (bank[5], bank[7])
        FRONT_AFTER = (1, 2, 3, 4, 5, 6)

        def flat(tile):
            return tile.rearrange("p t d -> p (t d)")

        block = ctx.enter_context(nc.Block())

        early, late = [], []
        early += [(ident[:, :], t["ident"])]
        for i, x in enumerate(("ln1_g", "ln1_b", "ln2_g", "ln2_b")):
            early.append((cols1[:, i:i + 1], t[x].rearrange("(d o) -> d o", o=1)))
        for a, loads in ((1, early), (2, late)):
            loads.append((w_qk[a][:, :, :], t[f"w_qk{a}"]))
            loads.append((rope[a][:, :, :], t[f"rope{a}"]))
            loads.append((w_v[a][:, :], t[f"w_v{a}"]))
            late.append((w_o[a][:, :], t[f"w_o{a}"]))
        late += [(ident_b[:, :], t["ident_b"]), (later_keys[:, :], t["later_keys"]),
                 (later_keys_T[:, :], t["later_keys_T"]), (iota_e[:, :], t["iota_e"]), (b_qk[:, :], t["b_qk"])]
        for i, x in enumerate(("bv", "bo", "b2")):
            late.append((rows[:, i, :], t[x].rearrange("(o d) -> o d", o=1)))
        late.append((rows[:, 4:4 + E, :], t["eb2"].rearrange("(o e) d -> o e d", o=1)))
        late.append((bg_row[:, :], t["bg"].rearrange("(o e) -> o e", o=1)))
        for i, x in enumerate(("g1", "be1", "g2", "be2")):
            late.append((ln_rows[:, i, :], t[x].rearrange("(o d) -> o d", o=1).broadcast_to([P, D])))
        late += [(w1[:, :], t["w1"]), (b1c[:, :], t["b1c"]), (w2[:, :, :], t["w2"].rearrange("(f p) d -> p f d", p=P)),
                 (wg[:, :], t["wg"]), (ew1[:, :, :], t["ew1"].rearrange("e d f -> d e f")), (eb1[:, :, :], t["eb1c"]),
                 (ew2[:, :, :, :], t["ew2"].rearrange("e (f p) d -> p e f d", p=P))]

        def ready(eng):
            eng.wait_ge(loaded, 16 * len(early))
            eng.wait_ge(set_up, 1)

        def all_ready(eng):
            eng.wait_ge(loaded_late, 16 * len(late))

        @block.sync
        def _(sp):
            for to, src in early:
                sp.dma_start(to, src).then_inc(loaded, 16)
            for to, src in late:
                sp.dma_start(to, src).then_inc(loaded_late, 16)
            for b, half, n in groups(sp):
                sp.wait_ge(f_outer.done, 5 * n + 5)
                sp.dma_start(tokens(x_ln_d, b, half), xb).then_inc(first["ln_out"], 16)
                proj[1].sp(sp, n, b, half)
            sp.wait_ge(first["ln_out"], 16 * B * HALVES)
            sp.wait_ge(proj[1].s["stored"], N_STORES * B * HALVES)
            barrier(sp, 1)
            attend[1].sp(sp)
            barrier(sp, 2)
            for b, half, n in groups(sp):
                sp.wait_ge(mid["x"], n + 1)
                sp.dma_start(tokens(x_mid_d, b, half), xf).then_inc(mid["out"], 16)
                sp.wait_ge(m_outer.done, 5 * n + 5)
                sp.dma_start(tokens(z_d, b, half), xz).then_inc(mid["out"], 16)
                proj[2].sp(sp, n, b, half)
            sp.wait_ge(mid["out"], 32 * B * HALVES)
            sp.wait_ge(proj[2].s["stored"], N_STORES * B * HALVES)
            barrier(sp, 3)
            attend[2].sp(sp)
            barrier(sp, 4)
            for b, half, n in groups(sp):
                sp.wait_ge(end["y"], n + 1)
                sp.dma_start(tokens(x_out, b, half), sums_of[half]).then_inc(end_out[half], 16)
            for half in range(HALVES):
                sp.wait_ge(end_out[half], 16 * B)

        @block.gpsimd
        def _(pool):
            pool.memset(q_work[:, :, :, :], 0.0)
            for i in range(QB):
                pool.memset(v_ones[i][:, :, :, :], 1.0)
            pool.memset(ones_row[:, :], 1.0)
            pool.memset(eps_col[:, :], EPS)
            pool.memset(e_base[:, :], float(np.exp(1.0)))
            pool.memset(minus_half[:, :], -0.5).then_inc(set_up, 1)
            ready(pool)
            for b, half, n in groups(pool):
                pool.wait_ge(f_outer.done, 5 * n)
                pool.dma_start(xt, tokens(x_in, b, half)).then_inc(first["x_in"], 16)
                f_outer.root(pool, n)
                f_inner.root(pool, n)
            barrier(pool, 1)
            all_ready(pool)
            attend[1].pool(pool)
            barrier(pool, 2)

            def load_mid(b, half, n):
                if not isinstance(n, int) or n:
                    pool.wait_ge(mid["x2"], n)
                if not isinstance(n, int) or n >= HALVES:
                    pool.wait_ge(mid["x"], n - 1)
                pool.dma_start(heads_in[:, :, :], dram["o1"][bass.ds(b * HG, HG), :, half * G:(half + 1) * G]
                               .rearrange("g p s -> p g s")).then_inc(mid["in"], 16)
                pool.dma_start(xb, tokens(x_ln_d, b, half)).then_inc(mid["in"], 16)
                pool.dma_start(x_ins[half], tokens(x_in, b, half)).then_inc(mid["in"], 16)

            load_mid(0, 0, 0)
            for (b, half, n), following in turns(pool):
                m_inner.root(pool, n)
                if following:
                    load_mid(*following)
                m_outer.root(pool, n)
            barrier(pool, 3)
            attend[2].pool(pool)
            barrier(pool, 4)

            def load(b, half, n):
                if not isinstance(n, int) or n:
                    pool.wait_ge(end["x1"], n)
                if not isinstance(n, int) or n >= HALVES:
                    pool.wait_ge(end["y"], n - 1)
                pool.dma_start(heads_in[:, :, :], dram["o2"][bass.ds(b * HG, HG), :, half * G:(half + 1) * G]
                               .rearrange("g p s -> p g s")).then_inc(end["in"], 16)
                pool.dma_start(xb, tokens(z_d, b, half)).then_inc(end["in"], 16)
                pool.dma_start(x_mids[half], tokens(x_mid_d, b, half)).then_inc(end["in"], 16)

            def front(n):
                e_first.root(pool, n)
                pool.wait_ge(end["gap"], n + 1)
                pool.tensor_tensor(e2[:, :], e_base[:, :], gap[:, :], ALU.pow).then_inc(end["e2"], 1)

            load(0, 0, 0)
            front(0)
            load(0, 1, 1)
            for (b, half, n), following in turns(pool):
                if following:
                    front(following[2])
                e_last.root(pool, n)
                if following and (not isinstance(b, int) or b < B - 1):
                    load(b + 1, half, n + HALVES)

        @block.tensor
        def _(pe):
            ready(pe)
            for b, half, n in groups(pe):
                proj[1].pe(pe, n, xz, f_inner.done, 5 * n + 5)
            barrier(pe, 1)
            all_ready(pe)
            attend[1].pe(pe)
            barrier(pe, 2)
            for b, half, n in groups(pe):
                pe.wait_ge(mid["in"], 48 * (n + 1))
                pe.wait_ge(mid["f"], n)
                pe.wait_ge(proj[2].s["products"], n)
                pe.wait_ge(mid["yT"], n)
                m_heads.pe(pe, n)
                pe.wait_ge(m_inner.done, 5 * n + 5)
                transposes(pe, bank[7], xd).then_inc(mid["T"], 1)
                pe.wait_ge(mid["yT"], n + 1)
                for f in range(FC):
                    pe.matmul(bank[f], w1[:, f * P:(f + 1) * P], yT[:, :], start=True, stop=True).then_inc(mid["up"], 1)
                pe.wait_ge(mid["gelu"], FC * (n + 1))
                down_product(pe, bank[6], 0, w2, rows[:, 2, :]).then_inc(mid["down"], 1)
                proj[2].pe(pe, n, xz, m_outer.done, 5 * n + 5)
            barrier(pe, 3)
            attend[2].pe(pe)
            barrier(pe, 4)

            def first_group(n):
                return isinstance(n, int) and n == 0

            def tokens_of_heads(half, n):
                pe.wait_ge(end["in"], 48 * (n + 1))
                for g in range(GT):
                    if g >= 2:
                        pe.wait_ge(end["normal"], GT * n + g - 1)
                    elif not first_group(n):
                        pe.wait_ge(end["gate" if g else "yT"], n)
                    for hg in range(HG):
                        last = pe.transpose(front_bank[g % 2][:, hg * P:(hg + 1) * P],
                                            heads_in[:, hg, g * P:(g + 1) * P], ident[:, :])
                    last.then_inc(end["tokens"], 1)

            def turn_heads(half, n):
                pe.wait_ge(end["normal"], GT * (n + 1))
                transposes(pe, front_bank[0], heads_tok).then_inc(end["T"], 1)

            def project_heads(half, n):
                pe.wait_ge(end["kept"], n + 1)
                for g in range(GT):
                    o = front_bank[1][:, g * P:(g + 1) * P]
                    pe.matmul(o, headsT[:, g * P:(g + 1) * P], w_o[2][:, :], start=True, stop=False)
                    last = pe.matmul(o, ones_row[:, :], rows[:, 1, :], start=False, stop=True)
                last.then_inc(end["product"], 1)

            def turn_input(half, n):
                pe.wait_ge(end["x1"], n + 1)
                transposes(pe, front_bank[0], x_ones[half]).then_inc(end["x1_T"], 1)

            def logits(half, n):
                pe.wait_ge(end["yT"], n + 1)
                for g in range(GT):
                    o = front_bank[1][:, g * E:(g + 1) * E]
                    pe.matmul(o, yTs[half][:, g * P:(g + 1) * P], wg[:, :], start=True, stop=False)
                    last = pe.matmul(o, ones_row[:, :], bg_row[:, :], start=False, stop=True)
                last.then_inc(end["logits"], 1)

            def up(half, n, e):
                for f in range(FC):
                    if e or not first_group(n):
                        pe.wait_ge(end["gelu"], FC * (E * n + e - 1) + f + 1)
                    pe.matmul(bank[f], ew1[:, e, f * P:(f + 1) * P], yTs[half][:, :], start=True,
                              stop=True).then_inc(end["up"], 1)

            def down(n, e):
                pe.wait_ge(end["gelu"], FC * (E * n + e + 1))
                if e >= 2 or not first_group(n):
                    pe.wait_ge(end["sum"], E * n + e - 1)
                down_product(pe, bank[4 + 2 * (e % 2)], e % 2, ew2[:, e, :, :],
                             rows[:, 4 + e, :]).then_inc(end["down"], 1)

            front = (tokens_of_heads, turn_heads, project_heads, None, turn_input, logits)
            for step in front:
                if step:
                    step(0, 0)
            up(0, 0, 0)
            for (b, half, n), following in turns(pe):
                for e in range(E):
                    if e + 1 < E:
                        up(half, n, e + 1)
                    elif following:
                        up(following[1], following[2], 0)
                    down(n, e)
                    if following and e in FRONT_AFTER and front[FRONT_AFTER.index(e)]:
                        front[FRONT_AFTER.index(e)](following[1], following[2])

        @block.vector
        def _(dve):
            ready(dve)

            def norms(n):
                dve.wait_ge(first["x_in"], 16 * (n + 1))
                f_outer.statistics(dve, n, xt)
                dve.wait_ge(first["ln_out"], 16 * n)
                f_outer.apply(dve, n, xb, xt)
                dve.wait_ge(f_outer.done, 5 * n + 5)
                f_inner.statistics(dve, n, xb)
                dve.wait_ge(proj[1].s["zT"], n)
                f_inner.apply(dve, n, xz, xb)

            norms(0)
            for (b, half, n), following in turns(dve):
                proj[1].dve_tokens(dve, n)
                if following:
                    norms(following[2])
                proj[1].dve_parts(dve, n, half)
            barrier(dve, 1)
            all_ready(dve)
            attend[1].dve(dve)
            barrier(dve, 2)
            for b, half, n in groups(dve):
                dve.wait_ge(mid["in"], 48 * (n + 1))
                m_heads.dve(dve, n)
                dve.wait_ge(m_heads.s["product"], n + 1)
                dve.tensor_tensor(flat(xc), bank[6], flat(xb), ALU.add).then_inc(mid["x2"], 1)
                dve.wait_ge(mid["x2"], n + 1)
                m_inner.statistics(dve, n, xc)
                m_inner.apply(dve, n, xd, xc)
                dve.wait_ge(mid["T"], n + 1)
                dve.tensor_scalar(yT[:, :], bank[7], cols1[:, 2:3], cols1[:, 3:4], ALU.mult, ALU.add).then_inc(mid["yT"], 1)
                dve.wait_ge(mid["down"], n + 1)
                dve.tensor_tensor(flat(xe), bank[6], flat(xc), ALU.add).then_inc(mid["f"], 1)
                dve.wait_ge(mid["f"], n + 1)
                dve.wait_ge(mid["out"], 32 * n)
                dve.tensor_tensor(flat(xf), flat(xe), flat(x_ins[half]), ALU.add).then_inc(mid["x"], 1)
                dve.wait_ge(mid["x"], n + 1)
                m_outer.statistics(dve, n, xf)
                dve.wait_ge(proj[2].s["zT"], n)
                m_outer.apply(dve, n, xz, xf)
                proj[2].dve_tokens(dve, n)
                proj[2].dve_parts(dve, n, half)
            barrier(dve, 3)
            attend[2].dve(dve)
            barrier(dve, 4)
            FRONT_LINKS, TAIL_LINKS = 11, 2
            links = {"front_link": [0, FRONT_LINKS], "tail_link": [0, TAIL_LINKS]}

            def link(ins, name, n):
                count, each = links[name]
                links[name][0] = (count + 1) % each
                ins.then_inc(end[name], 1)
                dve.wait_ge(end[name], each * n + count + 1)

            def rows_of(i):
                return ln_rows[:, i:i + 1, :].broadcast_to([P, GT, D])

            def normalise_heads(half, n):
                for g in range(GT):
                    dve.wait_ge(end["tokens"], GT * n + g + 1)
                    view = front_bank[g % 2].rearrange("p (h c) -> p h c", h=H)
                    dve.reciprocal(sums_rcp[:, g, :], view[:, :, DH]).then_inc(end["rcp"], 1)
                    dve.wait_ge(end["rcp"], GT * n + g + 1)
                    dve.tensor_tensor(heads_tok[:, g, :].rearrange("p (h d) -> p h d", h=H), view[:, :, 0:DH],
                                      sums_rcp[:, g, :].rearrange("p (h o) -> p h o", o=1).broadcast_to([P, H, DH]),
                                      ALU.mult).then_inc(end["normal"], 1)

            def keep_heads(half, n):
                dve.wait_ge(end["T"], n + 1)
                dve.tensor_copy(headsT[:, :], front_bank[0]).then_inc(end["kept"], 1)

            def add_attention(half, n):
                dve.wait_ge(end["product"], n + 1)
                link(dve.tensor_tensor(flat(xc), front_bank[1], flat(xb), ALU.add), "front_link", n)
                e_first.statistics(dve, n, xc)

            def first_norm(half, n):
                e_first.apply(dve, n, xd, xc)
                dve.wait_ge(e_first.done, 5 * n + 5)
                link(dve.tensor_tensor(xe, xd, rows_of(0), ALU.mult), "front_link", n)
                dve.tensor_tensor(x_ones[half], xe, rows_of(1), ALU.add).then_inc(end["x1"], 1)

            def keep_input(half, n):
                dve.wait_ge(end["x1_T"], n + 1)
                if not isinstance(n, int) or n >= HALVES:
                    dve.wait_ge(end["up"], E * FC * (n - 1))
                dve.tensor_copy(yTs[half][:, :], front_bank[0]).then_inc(end["yT"], 1)

            def share(half, n):
                dve.wait_ge(end["logits"], n + 1)
                dve.tensor_copy(gate[:, :, :].rearrange("p t e -> p (t e)"), front_bank[1][:, 0:GT * E]).then_inc(end["gate"], 1)
                dve.wait_ge(end["gate"], n + 1)
                carry_wait(dve)
                for g in range(GT):
                    last = dve.max(top[:, g, :], gate[:, g, :])
                link(last, "front_link", n)
                carry_wait(dve)
                for g in range(GT):
                    last = dve.max_index(top_i[:, g, :], top[:, g, :], gate[:, g, :])
                link(last, "front_link", n)
                dve.tensor_tensor(gap[:, :], top[:, :, 1], top[:, :, 0], ALU.subtract).then_inc(end["gap"], 1)
                link(dve.tensor_copy(top_f[:, :, :], top_i[:, :, 0:2]), "front_link", n)
                dve.wait_ge(end["e2"], n + 1)
                link(dve.tensor_scalar(esum[:, :], e2[:, :], 1.0, 0.0, ALU.add, ALU.add), "front_link", n)
                link(dve.reciprocal(pw[:, :, 0], esum[:, :]), "front_link", n)
                link(dve.tensor_tensor(pw[:, :, 1], e2[:, :], pw[:, :, 0], ALU.mult), "front_link", n)
                for i in range(2):
                    for g in range(GT):
                        last = dve.tensor_scalar(comb[:, i, g, :], iota_e[:, :], top_f[:, g, i:i + 1], pw[:, g, i:i + 1],
                                                 ALU.is_equal, ALU.mult)
                    link(last, "front_link", n)
                link(dve.tensor_tensor(weights[:, half, :, :], comb[:, 0, :, :], comb[:, 1, :, :], ALU.add), "front_link", n)

            front = (normalise_heads, keep_heads, add_attention, first_norm, keep_input, share)
            for step in front:
                step(0, 0)
            for (b, half, n), following in turns(dve):
                to = sums_of[half]
                if not isinstance(b, int) or b:
                    dve.wait_ge(end_out[half], 16 * b)
                for e in range(E):
                    dve.wait_ge(end["down"], E * n + e + 1)
                    if e:
                        dve.wait_ge(end["sum"], E * n + e)
                    for g in range(GT):
                        last = dve.scalar_tensor_tensor(to[:, g, :], bank[4 + 2 * (e % 2)][:, g * P:(g + 1) * P],
                                                        weights[:, half, g, e:e + 1], (to if e else x_ones[half])[:, g, :],
                                                        ALU.mult, ALU.add)
                    last.then_inc(end["sum"], 1)
                    if following and e in FRONT_AFTER:
                        front[FRONT_AFTER.index(e)](following[1], following[2])
                dve.wait_ge(end["sum"], E * (n + 1))
                e_last.statistics(dve, n, to)
                e_last.apply(dve, n, xz, to)
                dve.wait_ge(e_last.done, 5 * n + 5)
                link(dve.tensor_tensor(tail_a, xz, rows_of(2), ALU.mult), "tail_link", n)
                link(dve.tensor_tensor(tail_b, tail_a, rows_of(3), ALU.add), "tail_link", n)
                dve.tensor_tensor(flat(to), flat(tail_b), flat(x_mids[half]), ALU.add).then_inc(end["y"], 1)
            assert not any(count for count, _ in links.values())

        @block.scalar
        def _(act):
            ready(act)
            for b, half, n in groups(act):
                proj[1].act(act, n, b, half)
            barrier(act, 1)
            all_ready(act)
            attend[1].act(act)
            barrier(act, 2)
            for b, half, n in groups(act):
                for f in range(FC):
                    act.wait_ge(mid["up"], FC * n + f + 1)
                    act.wait_ge(mid["down"], n)
                    act.activation(hidden[:, 0, f, :], bank[f], ACT.Gelu, bias=b1c[:, f:f + 1]).then_inc(mid["gelu"], 1)
                proj[2].act(act, n, b, half)
            barrier(act, 3)
            attend[2].act(act)
            barrier(act, 4)
            for b, half, n in groups(act):
                for e in range(E):
                    for f in range(FC):
                        act.wait_ge(end["up"], FC * (E * n + e) + f + 1)
                        if e >= 2 or not isinstance(n, int) or n:
                            act.wait_ge(end["down"], E * n + e - 1)
                        act.activation(hidden[:, e % 2, f, :], bank[f], ACT.Gelu,
                                       bias=eb1[:, e, f:f + 1]).then_inc(end["gelu"], 1)


def _rope_tables(half_split):
    inv = (np.float32(10000.0) ** (-(np.arange(0, DH, 2, dtype=np.float32) / np.float32(DH)))).astype(np.float32)
    theta = np.arange(S, dtype=np.float32)[:, None] * inv[None, :]
    table = np.zeros((P, 2, S), np.float32)
    for r in range(P):
        d = r % 32 % 16 // 2
        angle, negative = (d % (DH // 2), d < DH // 2) if half_split else (d // 2, d % 2 == 0)
        table[r, 0] = np.cos(theta[:, angle])
        table[r, 1] = np.sin(theta[:, angle]) * np.float32(-1 if negative else 1)
    return table


def _columns(half_split):
    own, partner = [], []
    for r in range(P):
        hg, par, d, pair = r // 32, r % 32 // 16, r % 16 // 2, r % 2
        head = hg * HG + pair * 2 + par
        own.append(head * DH + d)
        partner.append(head * DH + ((d + DH // 2) % DH if half_split else d ^ 1))
    return own, partner


def kernel(**inputs):
    import concourse.bacc as bacc
    from concourse.bass_utils import run_bass_kernel_spmd

    a = {k.replace("L0_", ""): np.asarray(v) for k, v in inputs.items()}
    bf = mybir.dt.np(BF16)
    heads = np.arange(P)
    later = np.where(heads[None, :] > heads[:, None], LOW, 0.0)
    arrays = {
        "x": a["attn_x"],
        "ident": np.eye(P, dtype=np.float32), "ident_b": np.eye(P).astype(bf),
        "later_keys": later.astype(bf), "later_keys_T": later.T.astype(bf),
        "iota_e": np.tile(np.arange(E, dtype=np.float32), (P, 1)),
        "rope1": _rope_tables(False), "rope2": _rope_tables(True),
    }
    own, partner = _columns(False)
    q, k, v = (a["attn_Wqkv"][:, i * D:(i + 1) * D] for i in range(3))
    arrays["w_qk1"] = np.stack([q[:, own], q[:, partner], k[:, own], k[:, partner]], axis=1)
    arrays["w_v1"] = v
    own, partner = _columns(True)
    q, k = a["ffn_Wq"], a["ffn_Wk"]
    arrays["w_qk2"] = np.stack([q[:, own], q[:, partner], k[:, own], k[:, partner]], axis=1)
    q, k = a["ffn_bq"], a["ffn_bk"]
    arrays["b_qk"] = np.stack([q[own], q[partner], k[own], k[partner]], axis=1)
    arrays["w_v2"] = a["ffn_Wv"]
    arrays["w_o1"], arrays["w_o2"] = a["attn_Wo"], a["ffn_Wo"]
    for x in ("ln1_g", "ln1_b", "ln2_g", "ln2_b"):
        arrays[x] = a["attn_" + x]
    for x, y in (("bv", "bv"), ("bo", "bo"), ("bg", "bg"), ("wg", "Wg"), ("g1", "g1"), ("be1", "be1"), ("g2", "g2"),
                 ("be2", "be2"), ("ew1", "W1"), ("ew2", "W2"), ("eb2", "b2")):
        arrays[x] = a["ffn_" + y]
    arrays["w1"], arrays["w2"], arrays["b2"] = a["attn_W1"], a["attn_W2"], a["attn_b2"]
    arrays["b1c"] = a["attn_b1"].reshape(FC, P).T
    arrays["eb1c"] = a["ffn_b1"].reshape(E, FC, P).transpose(2, 0, 1)
    arrays = {f"in_{k}": np.ascontiguousarray(v) for k, v in arrays.items()}

    nc = bacc.Bacc("TRN2", target_bir_lowering=False, num_devices=1)
    t = {k[3:]: nc.dram_tensor(k, v.shape, mybir.dt.from_np(v.dtype), kind="ExternalInput").ap() for k, v in arrays.items()}
    out = nc.dram_tensor("out_x", (B, S, D), F32, kind="ExternalOutput").ap()
    build(nc, t, out)
    return run_bass_kernel_spmd(nc, [arrays], core_ids=[0]).results[0]["out_x"]
```
